# Optimizing a Trainium2 kernel written in Bass

```python
import numpy as np
import jax
import jax.numpy as jnp

def _softmax(x, axis=-1):
    return jax.nn.softmax(x, axis=axis)

def _gelu(x):
    return jax.nn.gelu(x, approximate=True)

def _silu(x):
    return jax.nn.silu(x)

def _sigmoid(x):
    return jax.nn.sigmoid(x)

def _layernorm(x, axis=-1, eps=1e-05):
    m = jnp.mean(x, axis=axis, keepdims=True)
    v = jnp.var(x, axis=axis, keepdims=True)
    return (x - m) / jnp.sqrt(v + eps)

def _scatter_add(tgt, idx, src, axis=0):
    return tgt.at[idx].add(src)

def _segment_sum(src, seg, n):
    return jax.ops.segment_sum(src, seg, n)
kernel_name = 'mk_flamingo_gated_d2_seqx_r8_2ea24b'

def setup_inputs(seed: int=0):
    np.random.seed(seed)
    _w = jnp.asarray

    def _rec_inputs():
        import jax
        import jax.numpy as jnp
        _rk = jax.random.key(seed)
        x = -0.0003929 + 0.9999 * jax.random.normal(jax.random.fold_in(_rk, 1), (32, 56, 128), jnp.float32)
        _lenS = 56 - jax.random.randint(jax.random.fold_in(_rk, 7), (32,), 0, max(1, 56 // 4) + 1, jnp.int32)
        _lenS2 = 1500 - jax.random.randint(jax.random.fold_in(_rk, 8), (32,), 0, max(1, 1500 // 4) + 1, jnp.int32)
        _ctx_768P = jax.random.normal(jax.random.fold_in(_rk, 11), (32, 16, 96), jnp.float32)
        _ctx_768c = jax.random.dirichlet(jax.random.fold_in(_rk, 511), 0.3 * jnp.ones((16,), jnp.float32), (32, 1500))
        _ctx_768t = jnp.einsum('bsk,bkd->bsd', _ctx_768c, _ctx_768P)
        _ctx_768t = _ctx_768t * jax.lax.rsqrt(jnp.mean(jnp.square(_ctx_768t)) + 1e-12) * 0.953939
        ctx_768 = -7.36909e-05 + 0.999899 * (_ctx_768t + 0.3 * jax.random.normal(jax.random.fold_in(_rk, 611), (32, 1500, 96), jnp.float32))
        _g = jax.random.normal(jax.random.fold_in(_rk, 9001), (2, 2), jnp.float32)
        _g = jnp.sign(_g) * jnp.maximum(jnp.abs(_g), 1.0) + (_g == 0) * 1.0
        g_xattn = _g[0]
        g_ffn = _g[1]
        return (x, ctx_768, g_xattn, g_ffn)
    x, ctx_768, g_xattn, g_ffn = _rec_inputs()

    def _L0_xattn_setup():
        import jax, jax.numpy as jnp
        import numpy as np
        EPS = 1e-05

        def layernorm(x, g, b):
            mu = jnp.mean(x, axis=-1, keepdims=True)
            var = jnp.mean(jnp.square(x - mu), axis=-1, keepdims=True)
            return (x - mu) * jax.lax.rsqrt(var + EPS) * g + b
        key = jax.random.key(seed)
        ks = jax.random.split(key, 12)
        B, L1, L2 = (8, 256, 256)
        D1, D2, E = (128, 96, 128)
        s1, s2, se = (D1 ** (-0.5), D2 ** (-0.5), E ** (-0.5))
        return {'modality1': jax.random.normal(ks[0], (B, L1, D1), jnp.float32), 'modality2': jax.random.normal(ks[1], (B, L2, D2), jnp.float32), 'ln1_g': jnp.ones((D1,), jnp.float32), 'ln1_b': jnp.zeros((D1,), jnp.float32), 'ln2_g': jnp.ones((D2,), jnp.float32), 'ln2_b': jnp.zeros((D2,), jnp.float32), 'Wq': jax.random.normal(ks[2], (D1, E), jnp.float32) * s1, 'bq': jax.random.normal(ks[3], (E,), jnp.float32) * 0.01, 'Wk': jax.random.normal(ks[4], (D2, E), jnp.float32) * s2, 'bk': jax.random.normal(ks[5], (E,), jnp.float32) * 0.01, 'Wv': jax.random.normal(ks[6], (D2, E), jnp.float32) * s2, 'bv': jax.random.normal(ks[7], (E,), jnp.float32) * 0.01, 'Wo': jax.random.normal(ks[8], (E, D1), jnp.float32) * se, 'bo': jax.random.normal(ks[9], (D1,), jnp.float32) * 0.01}
    _L0_xattn_all = _L0_xattn_setup()
    _L0_xattn_in = {k: v for k, v in _L0_xattn_all.items() if k in ('ln1_g', 'ln1_b', 'ln2_g', 'ln2_b', 'Wq', 'bq', 'Wk', 'bk', 'Wv', 'bv', 'Wo', 'bo')}
    del _L0_xattn_all

    def _L0_ffn_setup():
        import jax, jax.numpy as jnp
        import numpy as np
        import math
        D_IN = 128
        FEATURES = (512, 512, 128)
        BATCH, SEQ = (8, 256)

        def _conn_dense(kernel_bool, x):
            w = jnp.where(kernel_bool, jnp.float32(1.0), jnp.float32(-1.0))
            return x @ w
        key = jax.random.key(seed)
        kx, kk0, kk1, kk2 = jax.random.split(key, 4)
        x = jax.random.normal(kx, (BATCH, SEQ, D_IN), dtype=jnp.float32)
        k0 = jax.random.randint(kk0, (2 * D_IN, FEATURES[0]), 0, 2).astype(jnp.bool_)
        k1 = jax.random.randint(kk1, (FEATURES[0], FEATURES[1]), 0, 2).astype(jnp.bool_)
        k2 = jax.random.randint(kk2, (FEATURES[1], FEATURES[2]), 0, 2).astype(jnp.bool_)
        s0 = jnp.asarray(1.0 / math.sqrt(2 * D_IN), dtype=jnp.float32)
        s1 = jnp.asarray(1.0 / math.sqrt(FEATURES[0]), dtype=jnp.float32)
        s2 = jnp.asarray(1.0 / math.sqrt(FEATURES[1]), dtype=jnp.float32)
        return {'x': x, 'k0': k0, 'k1': k1, 'k2': k2, 's0': s0, 's1': s1, 's2': s2}
    _L0_ffn_all = _L0_ffn_setup()
    _L0_ffn_in = {k: v for k, v in _L0_ffn_all.items() if k in ('k0', 'k1', 'k2', 's0', 's1', 's2')}
    del _L0_ffn_all

    def _L1_xattn_setup():
        import jax, jax.numpy as jnp
        import numpy as np
        HEADS = 16
        DIM_HEAD = 64
        key = jax.random.key(seed)
        ks = jax.random.split(key, 7)
        B, Nq, Dq = (4, 256, 128)
        Nk, Dc = (128, 96)
        inner = HEADS * DIM_HEAD
        sq = 1.0 / np.sqrt(Dq)
        sc = 1.0 / np.sqrt(Dc)
        si = 1.0 / np.sqrt(inner)
        return {'x': jax.random.normal(ks[0], (B, Nq, Dq), dtype=jnp.float32), 'context': jax.random.normal(ks[1], (B, Nk, Dc), dtype=jnp.float32), 'Wq': jax.random.normal(ks[2], (Dq, inner), dtype=jnp.float32) * sq, 'Wk': jax.random.normal(ks[3], (Dc, inner), dtype=jnp.float32) * sc, 'Wv': jax.random.normal(ks[4], (Dc, inner), dtype=jnp.float32) * sc, 'Wo': jax.random.normal(ks[5], (inner, Dq), dtype=jnp.float32) * si, 'bo': jax.random.normal(ks[6], (Dq,), dtype=jnp.float32) * 0.01}
    _L1_xattn_all = _L1_xattn_setup()
    _L1_xattn_in = {k: v for k, v in _L1_xattn_all.items() if k in ('Wq', 'Wk', 'Wv', 'Wo', 'bo')}
    del _L1_xattn_all

    def _L1_ffn_setup():
        import jax, jax.numpy as jnp
        import numpy as np
        H = 128
        M = 64
        E = 16
        TOP_K = 4
        N_GROUP = 4
        TOPK_GROUP = 2
        SCALE = 2.5
        B, S = (2, 128)

        def _gate(x2d, gate_kernel, gate_bias):
            n = x2d.shape[0]
            logits = jnp.dot(x2d.astype(jnp.float32), gate_kernel.astype(jnp.float32))
            scores = jax.nn.sigmoid(logits)
            scores_for_choice = scores + gate_bias
            group_scores = scores_for_choice.reshape(n, N_GROUP, E // N_GROUP)
            top2 = jax.lax.top_k(group_scores, k=2)[0]
            group_sum = jnp.sum(top2, axis=-1)
            group_idx = jax.lax.top_k(group_sum, k=TOPK_GROUP)[1]
            group_mask = jnp.zeros_like(group_sum).at[jnp.arange(n)[:, None], group_idx].set(1.0)
            score_mask = jnp.repeat(group_mask[:, :, None], E // N_GROUP, axis=2).reshape(n, E)
            masked_scores = jnp.where(score_mask > 0, scores_for_choice, 0.0)
            topk_weight, topk_idx = jax.lax.top_k(masked_scores, k=TOP_K)
            topk_weight = topk_weight / (jnp.sum(topk_weight, axis=-1, keepdims=True) + 1e-20)
            topk_weight = topk_weight * SCALE
            return (topk_idx, topk_weight)
        key = jax.random.key(seed)
        ks = jax.random.split(key, 9)
        sc_h = 1.0 / np.sqrt(H)
        sc_m = 1.0 / np.sqrt(M)
        return {'hidden_states': jax.random.normal(ks[0], (B, S, H), jnp.float32), 'gate_kernel': jax.random.normal(ks[1], (H, E), jnp.float32) * sc_h, 'gate_bias': jax.random.normal(ks[2], (E,), jnp.float32) * 0.01, 'w_gate': jax.random.normal(ks[3], (E, H, M), jnp.float32) * sc_h, 'w_up': jax.random.normal(ks[4], (E, H, M), jnp.float32) * sc_h, 'w_down': jax.random.normal(ks[5], (E, M, H), jnp.float32) * sc_m, 'sw_gate': jax.random.normal(ks[6], (H, 2 * M), jnp.float32) * sc_h, 'sw_up': jax.random.normal(ks[7], (H, 2 * M), jnp.float32) * sc_h, 'sw_down': jax.random.normal(ks[8], (2 * M, H), jnp.float32) * (1.0 / np.sqrt(2 * M))}
    _L1_ffn_all = _L1_ffn_setup()
    _L1_ffn_in = {k: v for k, v in _L1_ffn_all.items() if k in ('gate_kernel', 'gate_bias', 'w_gate', 'w_up', 'w_down', 'sw_gate', 'sw_up', 'sw_down')}
    del _L1_ffn_all
    return {'x': x, 'ctx_768': ctx_768, 'g_xattn': g_xattn, 'g_ffn': g_ffn, 'L0_xattn_ln1_g': _L0_xattn_in['ln1_g'], 'L0_xattn_ln1_b': _L0_xattn_in['ln1_b'], 'L0_xattn_ln2_g': _L0_xattn_in['ln2_g'], 'L0_xattn_ln2_b': _L0_xattn_in['ln2_b'], 'L0_xattn_Wq': _L0_xattn_in['Wq'], 'L0_xattn_bq': _L0_xattn_in['bq'], 'L0_xattn_Wk': _L0_xattn_in['Wk'], 'L0_xattn_bk': _L0_xattn_in['bk'], 'L0_xattn_Wv': _L0_xattn_in['Wv'], 'L0_xattn_bv': _L0_xattn_in['bv'], 'L0_xattn_Wo': _L0_xattn_in['Wo'], 'L0_xattn_bo': _L0_xattn_in['bo'], 'L0_ffn_k0': _L0_ffn_in['k0'], 'L0_ffn_k1': _L0_ffn_in['k1'], 'L0_ffn_k2': _L0_ffn_in['k2'], 'L0_ffn_s0': _L0_ffn_in['s0'], 'L0_ffn_s1': _L0_ffn_in['s1'], 'L0_ffn_s2': _L0_ffn_in['s2'], 'L1_xattn_Wq': _L1_xattn_in['Wq'], 'L1_xattn_Wk': _L1_xattn_in['Wk'], 'L1_xattn_Wv': _L1_xattn_in['Wv'], 'L1_xattn_Wo': _L1_xattn_in['Wo'], 'L1_xattn_bo': _L1_xattn_in['bo'], 'L1_ffn_gate_kernel': _L1_ffn_in['gate_kernel'], 'L1_ffn_gate_bias': _L1_ffn_in['gate_bias'], 'L1_ffn_w_gate': _L1_ffn_in['w_gate'], 'L1_ffn_w_up': _L1_ffn_in['w_up'], 'L1_ffn_w_down': _L1_ffn_in['w_down'], 'L1_ffn_sw_gate': _L1_ffn_in['sw_gate'], 'L1_ffn_sw_up': _L1_ffn_in['sw_up'], 'L1_ffn_sw_down': _L1_ffn_in['sw_down']}

def reference(x, ctx_768, g_xattn, g_ffn, L0_xattn_ln1_g, L0_xattn_ln1_b, L0_xattn_ln2_g, L0_xattn_ln2_b, L0_xattn_Wq, L0_xattn_bq, L0_xattn_Wk, L0_xattn_bk, L0_xattn_Wv, L0_xattn_bv, L0_xattn_Wo, L0_xattn_bo, L0_ffn_k0, L0_ffn_k1, L0_ffn_k2, L0_ffn_s0, L0_ffn_s1, L0_ffn_s2, L1_xattn_Wq, L1_xattn_Wk, L1_xattn_Wv, L1_xattn_Wo, L1_xattn_bo, L1_ffn_gate_kernel, L1_ffn_gate_bias, L1_ffn_w_gate, L1_ffn_w_up, L1_ffn_w_down, L1_ffn_sw_gate, L1_ffn_sw_up, L1_ffn_sw_down):
    import jax
    import jax.numpy as jnp

    def _L0_xattn_ref(modality1, modality2, ln1_g, ln1_b, ln2_g, ln2_b, Wq, bq, Wk, bk, Wv, bv, Wo, bo):
        import jax, jax.numpy as jnp
        import numpy as np
        EPS = 1e-05

        def layernorm(x, g, b):
            mu = jnp.mean(x, axis=-1, keepdims=True)
            var = jnp.mean(jnp.square(x - mu), axis=-1, keepdims=True)
            return (x - mu) * jax.lax.rsqrt(var + EPS) * g + b
        E = Wq.shape[1]
        scaling = E ** (-0.5)
        x1 = layernorm(modality1, ln1_g, ln1_b)
        x2 = layernorm(modality2, ln2_g, ln2_b)
        q = x1 @ Wq + bq
        k = x2 @ Wk + bk
        v = x2 @ Wv + bv
        scores = jnp.einsum('bqe,bke->bqk', q, k) * scaling
        attn = jax.nn.softmax(scores, axis=-1)
        ctx = jnp.einsum('bqk,bke->bqe', attn, v)
        return ctx @ Wo + bo

    def _L0_ffn_ref(x, k0, k1, k2, s0, s1, s2):
        import jax, jax.numpy as jnp
        import numpy as np
        import math
        D_IN = 128
        FEATURES = (512, 512, 128)
        BATCH, SEQ = (8, 256)

        def _conn_dense(kernel_bool, x):
            w = jnp.where(kernel_bool, jnp.float32(1.0), jnp.float32(-1.0))
            return x @ w
        h = jnp.concatenate([x, -x], axis=-1)
        h = s0 * _conn_dense(k0, h)
        h = jax.nn.relu(h) * 2
        h = s1 * _conn_dense(k1, h)
        h = jax.nn.relu(h) * 2
        h = s2 * _conn_dense(k2, h)
        return h

    def _L1_xattn_ref(x, context, Wq, Wk, Wv, Wo, bo):
        import jax, jax.numpy as jnp
        import numpy as np
        HEADS = 16
        DIM_HEAD = 64
        B, Nq, _ = x.shape
        Nk = context.shape[1]
        h, dh = (HEADS, DIM_HEAD)
        q = (x @ Wq).reshape(B, Nq, h, dh)
        k = (context @ Wk).reshape(B, Nk, h, dh)
        v = (context @ Wv).reshape(B, Nk, h, dh)
        scale = 1.0 / jnp.sqrt(jnp.asarray(dh, dtype=x.dtype))
        scores = jnp.einsum('bqhd,bkhd->bhqk', q, k) * scale
        attn = jax.nn.softmax(scores, axis=-1)
        out = jnp.einsum('bhqk,bkhd->bqhd', attn, v).reshape(B, Nq, h * dh)
        return out @ Wo + bo

    def _L1_ffn_ref(hidden_states, gate_kernel, gate_bias, w_gate, w_up, w_down, sw_gate, sw_up, sw_down):
        import jax, jax.numpy as jnp
        import numpy as np
        H = 128
        M = 64
        E = 16
        TOP_K = 4
        N_GROUP = 4
        TOPK_GROUP = 2
        SCALE = 2.5
        B, S = (2, 128)

        def _gate(x2d, gate_kernel, gate_bias):
            n = x2d.shape[0]
            logits = jnp.dot(x2d.astype(jnp.float32), gate_kernel.astype(jnp.float32))
            scores = jax.nn.sigmoid(logits)
            scores_for_choice = scores + gate_bias
            group_scores = scores_for_choice.reshape(n, N_GROUP, E // N_GROUP)
            top2 = jax.lax.top_k(group_scores, k=2)[0]
            group_sum = jnp.sum(top2, axis=-1)
            group_idx = jax.lax.top_k(group_sum, k=TOPK_GROUP)[1]
            group_mask = jnp.zeros_like(group_sum).at[jnp.arange(n)[:, None], group_idx].set(1.0)
            score_mask = jnp.repeat(group_mask[:, :, None], E // N_GROUP, axis=2).reshape(n, E)
            masked_scores = jnp.where(score_mask > 0, scores_for_choice, 0.0)
            topk_weight, topk_idx = jax.lax.top_k(masked_scores, k=TOP_K)
            topk_weight = topk_weight / (jnp.sum(topk_weight, axis=-1, keepdims=True) + 1e-20)
            topk_weight = topk_weight * SCALE
            return (topk_idx, topk_weight)
        orig_shape = hidden_states.shape
        x = hidden_states.reshape(-1, orig_shape[-1])
        topk_idx, topk_weight = _gate(x, gate_kernel, gate_bias)
        onehot = (topk_idx[:, :, None] == jnp.arange(E)[None, None, :]).astype(topk_weight.dtype)
        combine = jnp.einsum('nke,nk->ne', onehot, topk_weight)
        g = jnp.einsum('nh,ehm->enm', x, w_gate)
        u = jnp.einsum('nh,ehm->enm', x, w_up)
        inter = jax.nn.silu(g) * u
        y_e = jnp.einsum('enm,emh->enh', inter, w_down)
        y = jnp.einsum('ne,enh->nh', combine, y_e)
        shared = jnp.dot(jax.nn.silu(jnp.dot(x, sw_gate)) * jnp.dot(x, sw_up), sw_down)
        return (y + shared).reshape(orig_shape)
    x = x + jnp.tanh(g_xattn[0]) * _L0_xattn_ref(_layernorm(x, axis=-1), ctx_768, L0_xattn_ln1_g, L0_xattn_ln1_b, L0_xattn_ln2_g, L0_xattn_ln2_b, L0_xattn_Wq, L0_xattn_bq, L0_xattn_Wk, L0_xattn_bk, L0_xattn_Wv, L0_xattn_bv, L0_xattn_Wo, L0_xattn_bo)
    x = x + jnp.tanh(g_ffn[0]) * _L0_ffn_ref(_layernorm(x, axis=-1), L0_ffn_k0, L0_ffn_k1, L0_ffn_k2, L0_ffn_s0, L0_ffn_s1, L0_ffn_s2)
    x = x + jnp.tanh(g_xattn[1]) * _L1_xattn_ref(_layernorm(x, axis=-1), ctx_768, L1_xattn_Wq, L1_xattn_Wk, L1_xattn_Wv, L1_xattn_Wo, L1_xattn_bo)
    x = x + jnp.tanh(g_ffn[1]) * _L1_ffn_ref(_layernorm(x, axis=-1), L1_ffn_gate_kernel, L1_ffn_gate_bias, L1_ffn_w_gate, L1_ffn_w_up, L1_ffn_w_down, L1_ffn_sw_gate, L1_ffn_sw_up, L1_ffn_sw_down)
    return x

_drawn_inputs = setup_inputs


def setup_inputs(seed=0):
    import zlib

    import numpy as np

    out = dict(_drawn_inputs(seed))
    spreads = {'g_ffn': (-1.0, 0.2),
     'L0_xattn_ln1_g': (1.0, 0.2),
     'L0_xattn_ln1_b': (0.0, 0.1),
     'L0_xattn_ln2_g': (1.0, 0.2),
     'L0_xattn_ln2_b': (0.0, 0.1)}
    factors = {'L0_xattn_bq': 5.281, 'L0_xattn_bk': 8.0, 'L1_xattn_bo': 3.025}
    for name, (base, spread) in spreads.items():
        noise = np.random.default_rng([zlib.crc32(name.encode()), seed]).standard_normal(out[name].shape)
        drawn = base * np.exp(spread * noise) if base else spread * noise
        out[name] = jnp.asarray(drawn.astype(out[name].dtype))
    for name, factor in factors.items():
        out[name] = (out[name] * factor).astype(out[name].dtype)
    return out
```

```python
import concourse.bass as bass
from concourse import mybir
from contextlib import ExitStack


def flamingo_two_layer_kernel(nc, a, out):
    fp32, bf16, fp16, u8 = mybir.dt.float32, mybir.dt.bfloat16, mybir.dt.float16, mybir.dt.uint8
    ALU = mybir.AluOpType
    ACT = mybir.ActivationFunctionType
    AX = mybir.AxisListType

    NB, S, D = a["x"].shape
    NK, C = a["ctx_768"].shape[1:]
    C1 = C + 1
    TOK = NB * S
    G = 4
    GT = TOK // G
    GB = NB // G
    J = 12
    KP = NK // J
    H, DH = 16, 64
    HH = H // 2
    HQ = HH * S
    E0 = a["L0_xattn_Wq"].shape[1]
    MT = 112
    NT = GT // MT
    KC = NK // 3
    FF = a["L0_ffn_k1"].shape[0]
    FT = FF // 128
    NE = a["L1_ffn_w_gate"].shape[0]
    ME = a["L1_ffn_w_gate"].shape[2]
    NP = NE // 2
    EPS = 1e-05
    NGATE = 27
    MAXAT = [(0, 1), (2,), (3, 4), (5,), (6, 7), (8,), (9, 10), (11,), (), (), (), ()]
    ORDER = [NP] + list(range(NP))
    UN = 2 * J
    NATW = C1 + 1

    ctx = ExitStack()
    with ctx:
        def sb(name, shape, dt=fp32):
            return ctx.enter_context(nc.sbuf_tensor(name, shape, dt))

        def sem(name):
            return ctx.enter_context(nc.semaphore(name))

        def wait(eng, s, value):
            if not isinstance(value, int) or value > 0:
                eng.wait_ge(s, value)

        ps = ctx.enter_context(nc.psum_tensor("ps", [128, 8, 512], fp32))

        def bank16(n, dt):
            return ps[:, n, :].bitcast(dt)

        AU = sb("AU", [128, NB, 2, HQ])
        AUhi = AU[:, :, :, :].bitcast(bf16)
        AUlo = AU[:, :, :, :].bitcast(fp16)
        AUflat = AU[:, :, :, :].rearrange("p b h q -> p (b h q)")
        xT = sb("xT", [128, TOK])
        xc = sb("xc", [128, GT])
        sqv = sb("sqv", [128, GT])
        rstd = sb("rstd", [MT, NT])
        xn = sb("xn", [128, GT])
        work = sb("work", [128, 2 * J * C + 4 * (J * NATW // 2) + 4 * (J * 128 // 2) + 4 * HQ + 4 * (HQ // 2)])

        def carver(flat, at):
            pos = [at]

            def carve(words, dt=fp32, rows=128):
                v = flat[0:rows, pos[0]:pos[0] + words]
                pos[0] += words
                return v if dt == fp32 else v.bitcast(dt)
            return carve

        carve = carver(work[:, :], 0)
        raw = [carve(J * C, rows=KP) for _ in range(2)]
        nat_hi = [carve(J * NATW // 2, bf16, KP).rearrange("p (j c) -> p j c", j=J) for _ in range(2)]
        nat_lo = [carve(J * NATW // 2, fp16, KP).rearrange("p (j c) -> p j c", j=J) for _ in range(2)]
        T_hi = [carve(J * 64, bf16).rearrange("p (j k) -> p j k", j=J) for _ in range(2)]
        T_lo = [carve(J * 64, fp16).rearrange("p (j k) -> p j k", j=J) for _ in range(2)]
        P = [carve(HQ, rows=KP) for _ in range(4)]
        P_lo = [carve(HQ // 2, fp16, KP) for _ in range(4)]
        carve = carver(work[:, :], 0)
        un = [carve(GT) for _ in range(2)]
        ydm = carve(GT)
        tnh = [carve(GT) for _ in range(2)]
        zg = tnh
        zu = [carve(GT) for _ in range(2)]
        inter = [carve(GT) for _ in range(2)]
        combT = carve(GT, rows=NE)
        pairsel = carve(NP * 128, rows=NE).rearrange("p (t m) -> p t m", t=NP)
        ost = carve(NT * 128, rows=MT).rearrange("p (t d) -> p t d", t=NT)
        gw = {n: carve(k, rows=MT) for n, k in dict(
            e1=64, sc=64, sfc=64, gt=1024, eq=1024, rank=64, sel=64, top=16, grank=16, gm=16,
            msk=64, w=64, ws=4, r=4, comb=64).items()}

        SLOT = 2 * HQ
        carve = carver(AUflat, 0)
        wq1 = carve(H * DH)
        wk1 = carve(H * DH, rows=C)
        wv1 = carve(H * DH, rows=C)
        wo1 = carve(HH * D).rearrange("p (t d) -> p t d", t=HH)
        wqT = carve(HH * 128).rearrange("p (t d) -> p t d", t=HH)
        wkT = carve(HH * C).rearrange("p (t c) -> p t c", t=HH)
        wvT = carve(HH * C).rearrange("p (t c) -> p t c", t=HH)
        xnat = carve(14 * 128).rearrange("p (t d) -> p t d", t=14)
        k0u = carve(2 * FF // 4, u8).rearrange("p (i f) -> p i f", i=2)
        k1u = carve(FT * FF // 4, u8).rearrange("p (i f) -> p i f", i=FT)
        k2u = carve(FT * 128 // 4, u8).rearrange("p (i f) -> p i f", i=FT)
        carve = carver(AUflat, 3 * GB * SLOT)
        U0 = carve(TOK, rows=C1)
        A0_hi = carve((TOK + 128) // 2, bf16)
        A0_lo = carve((TOK + 128) // 2, fp16)
        hf = AUflat[:, 3 * GB * SLOT + TOK:][:, 0:FT * GT].rearrange("p (m q) -> p m q", m=FT)
        hlo = carve(FT * GT // 2, fp16).rearrange("p (m q) -> p m q", m=FT)
        xh = carve(GT // 2, bf16)
        xl = carve(GT // 2, fp16)
        qT = carve(GT)
        yb = carve(GT)

        idf = sb("idf", [128, 128])
        idb = sb("idb", [128, 128], bf16)
        idh = sb("idh", [128, 128], fp16)
        mean_w = sb("mean_w", [128, 128])
        ones = sb("ones", [128, 128])
        spread = sb("spread", [C1, C])
        nhalf = sb("nhalf", [128, 1])
        lower = sb("lower", [MT, NE, NE])
        wq0 = sb("wq0", [128, E0])
        wk0 = sb("wk0", [C, E0])
        wkA = sb("wkA", [E0, C1])
        wv0 = sb("wv0", [C, E0])
        wvA = sb("wvA", [C, E0])
        bvA = sb("bvA", [E0, 1])
        wo0 = sb("wo0", [E0, D])
        Mh = sb("Mh", [D, H, C])
        Nh = sb("Nh", [C, H, D])
        w0 = sb("w0", [128, FF], bf16)
        w1 = sb("w1", [128, FT, FF], bf16)
        w2 = sb("w2", [128, FT, 128], bf16)
        gk = sb("gk", [D, NE])
        wg = sb("wg", [D, NE, ME])
        wu = sb("wu", [D, NE, ME])
        wd = sb("wd", [2 * ME, NP, D])
        sg = sb("sg", [D, 2 * ME])
        su = sb("su", [D, 2 * ME])
        sd = sb("sd", [2 * ME, D])
        rows = sb("rows", [1, 7 + NE])
        sc = sb("sc", [128, 7 + NE])
        sx = sb("sx", [128, 4])
        cols = sb("cols", [128, 10])
        ln1g, ln1b, ln2g, ln2b, bq0, bk0, bo0, bo1, bv0 = (cols[:, n:n + 1] for n in range(9))
        
        st = sb("st", [KP, J, 6])
        sm = sb("sm", [KP, 6, J])
        recip = sb("recip", [128, NB * 2 * HQ // 128])
        mx = sb("mx", [MT, NT, 3])
        mneg = sb("mneg", [MT, NT], bf16)
        mx0 = sb("mx0", [S, 3])
        mneg0 = sb("mneg0", [128, 1], bf16)

        names = """w_in pass const prep_pe prep_ev prep_misc gates
            ln_mean ln_xc ln_sq ln_var ln_ve ln_rs ln_bc ln_xn
            x1 q0 qT a0 a0hi a0lo
            stA smA rsA x2 natA_hi natA_lo fillA fevA maxA redA negA mtA rowA qkA expA ploA pvA uA
            sumB invB sumD invD recB bcB unB oB oTB yB ybB xB xhl h1 r1 hlo h2 r2 h3 aq ahi alo zrow
            natC_hi natC_lo fillC fevC maxC redC negC mtC rowC qkC expC ploC pvC uC
            sel recD bcD unD yh yD ydD xD lg ge gate cT cTs gu th zg zu cw moe dn fin tr ev out_done""".split()
        s = {n: sem("s_" + n) for n in names}
        s_rawA = [sem(f"s_rawA{n}") for n in range(2)]
        s_rawC = [sem(f"s_rawC{n}") for n in range(2)]

        ctx_v = a["ctx_768"].rearrange("b (p j) c -> b p (j c)", j=J)

        cvec = lambda n: a[n].rearrange("(p a) -> p a", a=1)
        rvec = lambda n: a[n].rearrange("(a p) -> a p", a=1)
        loads = [
            (xnat, a["x"].rearrange("b s d -> (b s) d").rearrange("(t p) d -> p t d", p=128)),
            (wq0[:, :], a["L0_xattn_Wq"]), (wk0[:, :], a["L0_xattn_Wk"]), (wv0[:, :], a["L0_xattn_Wv"]),
            (wo0[:, :], a["L0_xattn_Wo"]), (bv0, cvec("L0_xattn_bv")),
            (ln1g, cvec("L0_xattn_ln1_g")), (ln1b, cvec("L0_xattn_ln1_b")),
            (cols[0:C, 2:3], cvec("L0_xattn_ln2_g")), (cols[0:C, 3:4], cvec("L0_xattn_ln2_b")),
            (bq0, cvec("L0_xattn_bq")), (bk0, cvec("L0_xattn_bk")), (bo0, cvec("L0_xattn_bo")),
            (bo1, cvec("L1_xattn_bo")),
            (rows[:, 0:2], rvec("g_xattn")), (rows[:, 2:4], rvec("g_ffn")),
            (rows[:, 4:5], rvec("L0_ffn_s0")), (rows[:, 5:6], rvec("L0_ffn_s1")), (rows[:, 6:7], rvec("L0_ffn_s2")),
            (rows[:, 7:7 + NE], rvec("L1_ffn_gate_bias")),
        ]
        loads2 = [
            (wq1, a["L1_xattn_Wq"]), (wk1, a["L1_xattn_Wk"]), (wv1, a["L1_xattn_Wv"]),
            (wo1, a["L1_xattn_Wo"].rearrange("(t p) d -> p t d", p=128)),
            (k0u, a["L0_ffn_k0"].rearrange("(i p) f -> p i f", p=128)),
            (k1u, a["L0_ffn_k1"].rearrange("(i p) f -> p i f", p=128)),
            (k2u, a["L0_ffn_k2"].rearrange("(i p) f -> p i f", p=128)),
            (gk[:, :], a["L1_ffn_gate_kernel"]),
            (wg[:, :, :], a["L1_ffn_w_gate"].rearrange("e h m -> h e m")),
            (wu[:, :, :], a["L1_ffn_w_up"].rearrange("e h m -> h e m")),
            (wd[:, :, :], a["L1_ffn_w_down"].rearrange("(t e) m h -> (e m) t h", e=2)),
            (sg[:, :], a["L1_ffn_sw_gate"]), (su[:, :], a["L1_ffn_sw_up"]), (sd[:, :], a["L1_ffn_sw_down"]),
        ]
        NL = 16 * (len(loads) + len(loads2))

        block = ctx.enter_context(nc.Block())

        @block.sync
        def _(eng):
            for dst, src in loads:
                eng.dma_start(dst, src).then_inc(s["w_in"], 16)

            def load_a(b, k):
                wait(eng, s["natA_lo"], b - 1)
                eng.dma_start(raw[k], ctx_v[b]).then_inc(s_rawA[k], 16)
            load_a(0, 0)
            load_a(1, 1)
            with eng.Fori(1, NB // 2) as i:
                for k in range(2):
                    load_a(2 * i + k, k)

            eng.wait_ge(s["uA"], NB)
            sums = U0[C:C1, :].rearrange("a (p k) -> a p k", p=128)
            eng.dma_start(recip[:, 0:TOK // 128], sums).then_inc(s["sumB"], 16)
            eng.wait_ge(s["recB"], 1)
            eng.dma_start(sums, recip[:, 0:TOK // 128]).then_inc(s["invB"], 16)

            def load_c(b, k):
                wait(eng, s["natC_lo"], b - 1)
                eng.dma_start(raw[k], ctx_v[b]).then_inc(s_rawC[k], 16)
            eng.wait_ge(s["natA_lo"], NB)
            load_c(0, 0)
            load_c(1, 1)
            with eng.Fori(1, NB // 2) as i:
                for k in range(2):
                    load_c(2 * i + k, k)

            eng.wait_ge(s["uC"], 2 * NB)
            sums = AUflat[C:C1, :].rearrange("a (p k) -> a p k", p=128)
            eng.dma_start(recip[:, :], sums).then_inc(s["sumD"], 16)
            eng.wait_ge(s["recD"], 1)
            eng.dma_start(sums, recip[:, :]).then_inc(s["invD"], 16)

            out_v = out.rearrange("b s d -> (b s) d").rearrange("(g t p) d -> g p t d", t=NT, p=MT)
            with eng.Fori(0, G) as g:
                eng.wait_ge(s["ev"], g + 1)
                eng.dma_start(out_v[g], ost).then_inc(s["out_done"], 16)
            eng.wait_ge(s["out_done"], 16 * G)

        @block.gpsimd
        def _(eng):
            n = 0
            for t, v in ((ones, 1.0), (mean_w, 1.0 / D), (nhalf, -0.5)):
                eng.memset(t[:, :], v).then_inc(s["const"], 1)
                n += 1
            for t in (idf, idb, idh):
                eng.memset(t[:, :], 0.0).then_inc(s["const"], 1)
                n += 1
            eng.memset(lower[:, :, :], 1.0).then_inc(s["const"], 1)
            eng.memset(spread[:, :], 0.0).then_inc(s["const"], 1)
            for k in range(2):
                eng.memset(nat_hi[k][:, :, C:C1], 1.0).then_inc(s["const"], 1)
                eng.memset(nat_lo[k][:, :, C:C1], 0.0).then_inc(s["const"], 1)
                eng.memset(T_hi[k], 0.0).then_inc(s["const"], 1)
                eng.memset(T_lo[k], 0.0).then_inc(s["const"], 1)
            eng.memset(mneg0[:, :], 0.0).then_inc(s["const"], 1)
            eng.memset(A0_hi[:, TOK:TOK + 128], 0.0).then_inc(s["const"], 1)
            n += 1 + 1 + 8 + 2
            eng.wait_ge(s["const"], n)
            for t in (idf, idb, idh):
                eng.affine_select(out=t[:, :], in_=t[:, :], compare_op=ALU.not_equal, fill=1.0,
                                  base=0, pattern=[[-1, 128]], channel_multiplier=1).then_inc(s["const"], 1)
            eng.affine_select(out=spread[:, :], in_=spread[:, :], compare_op=ALU.not_equal, fill=1.0,
                              base=-C, pattern=[[0, C]], channel_multiplier=1).then_inc(s["const"], 1)
            eng.affine_select(out=lower[:, :, :], in_=lower[:, :, :], compare_op=ALU.is_ge, fill=0.0,
                              base=-1, pattern=[[1, NE], [-1, NE]], channel_multiplier=0)\
               .then_inc(s["const"], 1)
            def ln_power(n):
                eng.wait_ge(s["ln_ve"], n + 1)
                eng.tensor_tensor(rstd[:, :], rstd[:, :], nhalf[0:MT, :].to_broadcast([MT, NT]), ALU.pow)\
                   .then_inc(s["ln_rs"], 1)

            with eng.Fori(0, G) as g:
                ln_power(2 * g)
                ln_power(2 * g + 1)

            def rstd_a(b):
                eng.wait_ge(s["smA"], 7 * b + 7)
                eng.tensor_tensor(sm[:, 4, :], sm[:, 4, :], nhalf[0:KP, :].to_broadcast([KP, J]), ALU.pow).then_inc(s["rsA"], 1)

            def split(b, k, hi, lo):
                src = raw[k].rearrange("p (j c) -> p j c", j=J)
                eng.sem_inc(s["pass"], 1)
                eng.tensor_copy(nat_hi[k][:, :, 0:C], src).then_inc(hi, 1)
                eng.wait_ge(hi, b + 1)
                eng.tensor_tensor(nat_lo[k][:, :, 0:C], src, nat_hi[k][:, :, 0:C], ALU.subtract)\
                   .then_inc(lo, 1)

            def prep_a(b, k):
                rstd_a(b)
                eng.wait_ge(s["x2"], b + 1)
                wait(eng, s["pvA"], b - 1)
                split(b, k, s["natA_hi"], s["natA_lo"])
            prep_a(0, 0)
            prep_a(1, 1)
            with eng.Fori(1, NB // 2) as i:
                for k in range(2):
                    prep_a(2 * i + k, k)

            for g in range(G):
                ln_power(2 * G + 2 * g)
                eng.wait_ge(s["h3"], g + 1)
                eng.memset(AU[C:C1, g * GB:g * GB + GB, :, :].rearrange("p b h q -> p (b h q)"), 0.0)\
                   .then_inc(s["zrow"], 1)
                eng.wait_ge(s["zrow"], g + 1)
                ln_power(2 * G + 2 * g + 1)

            def prep_c(b, k):
                eng.wait_ge(s_rawC[k], 16 * (b // 2) + 16 if isinstance(b, int) else b * 8 + (16 - 8 * k))
                wait(eng, s["pvC"], UN * (b - 1))
                split(b, k, s["natC_hi"], s["natC_lo"])
            eng.wait_ge(s["pvA"], NB)
            prep_c(0, 0)
            prep_c(1, 1)
            with eng.Fori(1, NB // 2) as i:
                for k in range(2):
                    prep_c(2 * i + k, k)

            eng.wait_ge(s["pvC"], UN * NB)
            eng.memset(pairsel, 1.0).then_inc(s["sel"], 1)
            eng.wait_ge(s["sel"], 1)
            eng.affine_select(out=pairsel, in_=pairsel, compare_op=ALU.is_ge, fill=0.0,
                              base=0, pattern=[[128, NP], [1, 128]], channel_multiplier=-ME)\
               .then_inc(s["sel"], 1)
            eng.wait_ge(s["sel"], 2)
            eng.affine_select(out=pairsel, in_=pairsel, compare_op=ALU.is_ge, fill=0.0,
                              base=ME - 1, pattern=[[-128, NP], [-1, 128]], channel_multiplier=ME)\
               .then_inc(s["sel"], 1)
            eng.wait_ge(s["sel"], 3)
            with eng.Fori(0, G) as g:
                ln_power(4 * G + g)

        @block.scalar
        def _(eng):
            for dst, src in loads2:
                eng.dma_start(dst, src).then_inc(s["w_in"], 16)
            eng.wait_ge(s["w_in"], NL)
            eng.activation(rows[:, 0:4], rows[:, 0:4], ACT.Tanh).then_inc(s["gates"], 1)

            def ln_square(n):
                eng.wait_ge(s["ln_xc"], n + 1)
                eng.activation(sqv[:, :], xc[:, :], ACT.Square).then_inc(s["ln_sq"], 1)

            with eng.Fori(0, G) as g:
                ln_square(2 * g)
                ln_square(2 * g + 1)
                eng.wait_ge(s["q0"], g + 1)
                eng.activation(qT[:, :], ps[:, 2, 0:GT], ACT.Identity, bias=bq0).then_inc(s["qT"], 1)
                eng.wait_ge(s["a0"], g + 1)
                eng.activation(A0_hi[0:C1, bass.ds(g * GT, GT)], ps[0:C1, 3, 0:GT], ACT.Copy)\
                   .then_inc(s["a0hi"], 1)

            def fill_evac(src_bank, q, k, sig):
                T, dt = (T_hi, bf16) if q < 2 else (T_lo, fp16)
                src = bank16(src_bank, dt)[0:C1, 0:6 * 128].rearrange("p (j k) -> p j k", j=6)
                eng.activation(T[k][0:C1, 6 * (q % 2):6 * (q % 2) + 6, 0:KP], src[:, :, 0:KP], ACT.Copy)\
                   .then_inc(sig, 1)

            def fills_a(b, k):
                for q in range(4):
                    eng.wait_ge(s["fillA"], 4 * b + q + 1)
                    fill_evac((4, 7)[q % 2], q, k, s["fevA"])

            def body_a(b, k, more):
                for u in range(2):
                    eng.wait_ge(s["qkA"], 2 * b + u + 1)
                    wait(eng, s["pvA"], b - 1)
                    slot = 2 * k + u
                    eng.activation(P[slot][:, 0:6 * S], ps[0:KP, u, 0:6 * S], ACT.Exp).then_inc(s["expA"], 1)
                if more:
                    fills_a(b + 1, 1 - k)
                eng.wait_ge(s["pvA"], b + 1)
                eng.activation(U0[:, bass.ds(b * S, S)], ps[0:C1, 3, 0:S], ACT.Copy).then_inc(s["uA"], 1)
            fills_a(0, 0)
            body_a(0, 0, True)
            body_a(1, 1, True)
            with eng.Fori(1, NB // 2 - 1) as i:
                for k in range(2):
                    body_a(2 * i + k, k, True)
            body_a(NB - 2, 0, True)
            body_a(NB - 1, 1, False)

            with eng.Fori(0, G) as g:
                eng.wait_ge(s["oB"], g + 1)
                eng.activation(qT[:, :], ps[:, 2, 0:GT], ACT.Identity, bias=bvA[:, :]).then_inc(s["oTB"], 1)
                eng.wait_ge(s["yB"], g + 1)
                eng.activation(yb[:, :], ps[:, 3, 0:GT], ACT.Identity, bias=bo0).then_inc(s["ybB"], 1)
                ln_square(2 * G + 2 * g)
                for m in range(FT):
                    eng.wait_ge(s["h1"], FT * g + m + 1)
                    eng.activation(hf[:, m, :], ps[:, m, 0:GT], ACT.Relu, scale=sx[:, 0:1]).then_inc(s["r1"], 1)
                eng.wait_ge(s["h2"], g * FT + FT)
                for m in range(FT):
                    eng.activation(hf[:, m, :], ps[:, 4 + m, 0:GT], ACT.Relu, scale=sx[:, 1:2])\
                       .then_inc(s["r2"], 1)
                ln_square(2 * G + 2 * g + 1)
                for h in range(H):
                    eng.wait_ge(s["aq"], H * g + h + 1)
                    dst = AUhi[0:C, bass.ds(g * GB, GB), h // HH, (h % HH) * S:(h % HH) * S + S]
                    eng.activation(dst, ps[0:C, h % 4, 0:GT].rearrange("p (b q) -> p b q", b=GB), ACT.Copy)\
                       .then_inc(s["ahi"], 1)

            def u_evac(b, h):
                eng.wait_ge(s["pvC"], UN * b + J * (h + 1))
                eng.activation(AU[0:C1, b, h, :], ps[0:C1, 3 + h, 0:HQ], ACT.Copy).then_inc(s["uC"], 1)

            def body_c(b, k, first, last):
                for u in range(UN):
                    slot = u % 4
                    eng.wait_ge(s["qkC"], UN * b + u + 1)
                    wait(eng, s["pvC"], UN * b + u - 3)
                    eng.activation(P[slot][:, :], ps[0:KP, u % 3, 0:HQ], ACT.Exp).then_inc(s["expC"], 1)
                    if u == 2 and not first:
                        u_evac(b - 1, 1)
                    if u == J + 2:
                        u_evac(b, 0)
                    if 6 <= u < 10 and not last:
                        q = u - 6
                        eng.wait_ge(s["fillC"], 4 * (b + 1) + q + 1)
                        fill_evac(7, q, 1 - k, s["fevC"])
            for q in range(4):
                eng.wait_ge(s["fillC"], q + 1)
                fill_evac(7, q, 0, s["fevC"])
            body_c(0, 0, True, False)
            with eng.Fori(0, NB // 2 - 1) as i:
                body_c(2 * i + 1, 1, False, False)
                body_c(2 * i + 2, 0, False, False)
            body_c(NB - 1, 1, False, True)
            u_evac(NB - 1, 1)

            with eng.Fori(0, G) as g:
                eng.wait_ge(s["yh"], H * g + H)
                eng.activation(ydm, ps[:, 4, 0:GT], ACT.Identity, bias=bo1).then_inc(s["ydD"], 1)
                ln_square(4 * G + g)
                eng.wait_ge(s["lg"], g + 1)
                eng.activation(gw["e1"], ps[0:MT, 6, 0:NT * NE], ACT.Exp, scale=-1.0).then_inc(s["ge"], 1)
                for i in range(NP + 1):
                    eng.wait_ge(s["gu"], (NP + 1) * g + i + 1)
                    eng.activation(tnh[i % 2], ps[:, 3 * (i % 2), 0:GT], ACT.Tanh, scale=0.5)\
                       .then_inc(s["th"], 1)
                eng.wait_ge(s["tr"], g + 1)
                eng.activation(ost, ps[0:MT, 7, :].rearrange("p (t d) -> p t d", t=NT), ACT.Copy)\
                   .then_inc(s["ev"], 1)
                eng.wait_ge(s["out_done"], 16 * g + 16)

        @block.vector
        def _(eng):
            eng.wait_ge(s["w_in"], NL)
            ev = [0]

            def take():
                eng.wait_ge(s["prep_pe"], ev[0] + 1)
                ev[0] += 1
                return ps[:, ev[0] % 2, :]

            for t in range(4):
                n = min(4, 14 - 4 * t)
                eng.tensor_copy(xT[:, 512 * t:512 * t + 128 * n], take()[:, 0:128 * n]).then_inc(s["prep_ev"], 1)
            eng.tensor_copy(sc[:, :], take()[:, 0:7 + NE]).then_inc(s["prep_ev"], 1)
            eng.tensor_tensor(bvA[:, :], take()[:, 0:1], bv0, ALU.add).then_inc(s["prep_ev"], 1)
            eng.tensor_scalar(wvA[:, :], wv0[:, :], cols[0:C, 2:3], None, ALU.mult).then_inc(s["prep_misc"], 1)
            b = take()
            eng.tensor_scalar(wkA[:, C:C1], b[:, 0:1], bk0, float(E0) ** -0.5, ALU.add, ALU.mult)\
               .then_inc(s["prep_ev"], 1)
            eng.tensor_scalar(wk0[:, :], wk0[:, :], cols[0:C, 2:3], None, ALU.mult).then_inc(s["prep_misc"], 1)
            eng.tensor_scalar(wkA[:, 0:C], take()[:, 0:C], float(E0) ** -0.5, None, ALU.mult)\
               .then_inc(s["prep_ev"], 1)
            for dst, width in ((wqT, 128), (wkT, C), (wvT, C)):
                for t in range(HH // 4):
                    v = take()[:, 0:512].rearrange("p (t c) -> p t c", t=4)
                    eng.tensor_copy(dst[:, 4 * t:4 * t + 4, :], v[:, :, 0:width]).then_inc(s["prep_ev"], 1)
            for t in range(H // 4):
                v = take()[:, :].rearrange("p (t c) -> p t c", t=4)
                h0 = 8 * (t % 2) + t // 2
                eng.tensor_scalar(Mh[:, h0:h0 + 7:2, :], v[:, :, 0:C], float(DH) ** -0.5, None, ALU.mult)\
                   .then_inc(s["prep_ev"], 1)
            for t in range(H // 4):
                v = take()[0:C, :].rearrange("p (t c) -> p t c", t=4)
                h0 = 8 * (t % 2) + t // 2
                eng.tensor_copy(Nh[:, h0:h0 + 7:2, :], v).then_inc(s["prep_ev"], 1)
            eng.tensor_tensor(w0[:, :], k0u[:, 0, :], k0u[:, 1, :], ALU.subtract).then_inc(s["prep_misc"], 1)
            eng.tensor_scalar(w1[:, :, :], k1u, 2.0, -1.0, ALU.mult, ALU.add).then_inc(s["prep_misc"], 1)
            eng.tensor_scalar(w2[:, :, :], k2u, 2.0, -1.0, ALU.mult, ALU.add).then_inc(s["prep_misc"], 1)
            eng.wait_ge(s["prep_ev"], 5)
            eng.tensor_scalar(sx[:, 0:1], sc[:, 4:5], 4.0, None, ALU.mult).then_inc(s["prep_misc"], 1)
            eng.tensor_scalar(sx[:, 1:2], sc[:, 5:6], 2.0, None, ALU.mult).then_inc(s["prep_misc"], 1)
            eng.tensor_tensor(sx[:, 2:3], sc[:, 2:3], sc[:, 6:7], ALU.mult).then_inc(s["prep_misc"], 1)
            eng.wait_ge(s["prep_ev"], ev[0])
            eng.wait_ge(s["prep_misc"], 8)

            def layer_norm(n, src):
                eng.wait_ge(s["ln_mean"], n + 1)
                eng.tensor_tensor(xc[:, :], src, ps[:, 0, 0:GT], ALU.subtract).then_inc(s["ln_xc"], 1)
                eng.wait_ge(s["ln_var"], n + 1)
                eng.tensor_scalar(rstd[:, :], ps[0:MT, 1, 0:NT], EPS, None, ALU.add).then_inc(s["ln_ve"], 1)
                eng.wait_ge(s["ln_bc"], n + 1)
                eng.tensor_tensor(xn[:, :], xc[:, :], ps[:, 0, 0:GT], ALU.mult).then_inc(s["ln_xn"], 1)
                eng.wait_ge(s["ln_xn"], n + 1)

            with eng.Fori(0, G) as g:
                cs = bass.ds(g * GT, GT)
                layer_norm(2 * g, xT[:, cs])
                layer_norm(2 * g + 1, xn[:, :])
                eng.tensor_scalar(xn[:, :], xn[:, :], ln1g, ln1b, ALU.mult, ALU.add).then_inc(s["x1"], 1)
                eng.wait_ge(s["a0hi"], g + 1)
                eng.tensor_tensor(A0_lo[0:C1, cs], ps[0:C1, 3, 0:GT], A0_hi[0:C1, cs], ALU.subtract)\
                   .then_inc(s["a0lo"], 1)
                eng.wait_ge(s["a0lo"], g + 1)

            def stats(b, k):
                eng.wait_ge(s_rawA[k], 16 * (b // 2) + 16 if isinstance(b, int) else b * 8 + (16 - 8 * k))
                src = raw[k].rearrange("p (j c) -> p j c", j=J)
                for j in range(J):
                    eng.bn_stats(st[:, j, :], src[:, j, :]).then_inc(s["stA"], 1)
                eng.wait_ge(s["stA"], J * b + J)
                eng.tensor_tensor(sm[:, 0, :], st[:, :, 1], st[:, :, 4], ALU.add).then_inc(s["smA"], 1)
                eng.tensor_tensor(sm[:, 1, :], st[:, :, 1], st[:, :, 4], ALU.subtract).then_inc(s["smA"], 1)
                eng.tensor_tensor(sm[:, 2, :], st[:, :, 2], st[:, :, 5], ALU.add).then_inc(s["smA"], 1)
                eng.wait_ge(s["smA"], 7 * b + 3)
                eng.scalar_tensor_tensor(sm[:, 3, :], sm[:, 1, :], 0.25, sm[:, 1, :], ALU.mult, ALU.mult)\
                   .then_inc(s["smA"], 1)
                eng.tensor_scalar(sm[:, 4, :], sm[:, 2, :], 1.0 / C, EPS, ALU.mult, ALU.add)\
                   .then_inc(s["smA"], 1)
                eng.tensor_scalar(sm[:, 0, :], sm[:, 0, :], 0.5, None, ALU.mult).then_inc(s["smA"], 1)
                eng.wait_ge(s["smA"], 7 * b + 6)
                eng.tensor_tensor(sm[:, 4, :], sm[:, 4, :], sm[:, 3, :], ALU.add).then_inc(s["smA"], 1)

            def normalise(b, k):
                src = raw[k].rearrange("p (j c) -> p j c", j=J)
                eng.wait_ge(s["rsA"], b + 1)
                for j in range(J):
                    ins = eng.tensor_scalar(src[:, j, :], src[:, j, :], sm[:, 0, j:j + 1], sm[:, 4, j:j + 1],
                                            ALU.subtract, ALU.mult)
                ins.then_inc(s["x2"], 1)

            def maxima_a(b):
                for c in range(3):
                    eng.wait_ge(s["maxA"], 3 * b + c + 1)
                    eng.tensor_reduce(mx0[:, c:c + 1], ps[0:S, 5 + c % 2, 0:KC], AX.X, ALU.max)\
                       .then_inc(s["redA"], 1)
                eng.wait_ge(s["redA"], 3 * b + 3)
                wait(eng, s["mtA"], b)
                eng.tensor_reduce(mneg0[0:S, :], mx0[:, :], AX.X, ALU.max, negate=True).then_inc(s["negA"], 1)

            def row_a(b):
                eng.wait_ge(s["mtA"], b + 1)
                row = A0_hi[C:C1, bass.ds(b * S, S)]
                eng.tensor_tensor(row, bank16(2, bf16)[0:1, 0:S], row, ALU.add).then_inc(s["rowA"], 1)

            def body_a(b, k, more1, more2):
                if more2:
                    stats(b + 2, k)
                for u in range(2):
                    slot = 2 * k + u
                    eng.wait_ge(s["expA"], 2 * b + u + 1)
                    eng.tensor_tensor(P_lo[slot][:, 0:6 * S], P[slot][:, 0:6 * S],
                                      P[slot].bitcast(bf16)[:, 1:12 * S:2], ALU.subtract).then_inc(s["ploA"], 1)
                if more1:
                    maxima_a(b + 1)
                if more2:
                    normalise(b + 2, k)
                if more1:
                    row_a(b + 1)
            stats(0, 0)
            normalise(0, 0)
            stats(1, 1)
            normalise(1, 1)
            maxima_a(0)
            row_a(0)
            body_a(0, 0, True, True)
            body_a(1, 1, True, True)
            with eng.Fori(1, NB // 2 - 1) as i:
                for k in range(2):
                    body_a(2 * i + k, k, True, True)
            body_a(NB - 2, 0, True, False)
            body_a(NB - 1, 1, False, False)

            eng.wait_ge(s["sumB"], 16)
            eng.reciprocal(recip[:, 0:TOK // 128], recip[:, 0:TOK // 128]).then_inc(s["recB"], 1)
            with eng.Fori(0, G) as g:
                cs = bass.ds(g * GT, GT)
                eng.wait_ge(s["bcB"], g + 1)
                eng.tensor_tensor(xc[0:C, :], U0[0:C, cs], ps[0:C, 0, 0:GT], ALU.mult).then_inc(s["unB"], 1)
                eng.wait_ge(s["ybB"], g + 1)
                eng.scalar_tensor_tensor(xT[:, cs], yb[:, :], sc[:, 0:1], xT[:, cs], ALU.mult, ALU.add)\
                   .then_inc(s["xB"], 1)
                eng.wait_ge(s["xB"], 2 * g + 1)
                layer_norm(2 * G + 2 * g, xT[:, cs])
                eng.tensor_copy(xh[:, :], xn[:, :]).then_inc(s["xhl"], 1)
                eng.wait_ge(s["xhl"], 2 * g + 1)
                eng.tensor_tensor(xl[:, :], xn[:, :], xh[:, :], ALU.subtract).then_inc(s["xhl"], 1)
                for layer, r in (("h1", s["r1"]), ("h2", s["r2"])):
                    for m in range(FT):
                        eng.wait_ge(r, FT * g + m + 1)
                        eng.tensor_tensor(hlo[:, m, :], hf[:, m, :], hf[:, m, :].bitcast(bf16)[:, 1:2 * GT:2],
                                          ALU.subtract).then_inc(s["hlo"], 1)
                    if layer == "h1":
                        eng.wait_ge(s["h2"], FT * g + FT)
                eng.wait_ge(s["h3"], g + 1)
                eng.scalar_tensor_tensor(xT[:, cs], ps[:, 0, 0:GT], sx[:, 2:3], xT[:, cs], ALU.mult, ALU.add)\
                   .then_inc(s["xB"], 1)
                eng.wait_ge(s["xB"], 2 * g + 2)
                layer_norm(2 * G + 2 * g + 1, xT[:, cs])
                for h in range(H):
                    eng.wait_ge(s["ahi"], H * g + h + 1)
                    at = (h % HH) * S
                    bs = bass.ds(g * GB, GB)
                    eng.tensor_tensor(AUlo[0:C, bs, h // HH, HQ + at:HQ + at + S],
                                      ps[0:C, h % 4, 0:GT].rearrange("p (b q) -> p b q", b=GB),
                                      AUhi[0:C, bs, h // HH, at:at + S], ALU.subtract).then_inc(s["alo"], 1)

            def maximum(g, n):
                eng.wait_ge(s["maxC"], J * g + n + 1)
                eng.tensor_reduce(mx[:, n // 3, n % 3:n % 3 + 1], ps[0:MT, 5 + n % 2, 0:KC], AX.X, ALU.max)\
                   .then_inc(s["redC"], 1)

            def negate(g):
                eng.wait_ge(s["redC"], J * g + J)
                wait(eng, s["mtC"], g)
                eng.tensor_reduce(mneg[:, :], mx[:, :, :], AX.X, ALU.max, negate=True).then_inc(s["negC"], 1)

            def row_c(g, b, h):
                eng.wait_ge(s["mtC"], g + 1)
                eng.tensor_copy(AUhi[C:C1, b, h, 0:HQ], bank16(5, bf16)[0:1, 0:HQ]).then_inc(s["rowC"], 1)

            def body_c(b, k, last):
                for u in range(UN):
                    slot = u % 4
                    eng.wait_ge(s["expC"], UN * b + u + 1)
                    eng.tensor_tensor(P_lo[slot][:, :], P[slot][:, :], P[slot].bitcast(bf16)[:, 1:2 * HQ:2],
                                      ALU.subtract).then_inc(s["ploC"], 1)
                    h, j = u // J, u % J
                    if h == 1 and last:
                        continue
                    for n in MAXAT[j]:
                        maximum(2 * b + h + 1, n)
                    if j == 7:
                        negate(2 * b + h + 1)
                    if j == 9:
                        row_c(2 * b + h + 1, b + h, 1 - h)
            eng.wait_ge(s["zrow"], G)
            for n in range(J):
                maximum(0, n)
            negate(0)
            row_c(0, 0, 0)
            body_c(0, 0, False)
            with eng.Fori(0, NB // 2 - 1) as i:
                body_c(2 * i + 1, 1, False)
                body_c(2 * i + 2, 0, False)
            body_c(NB - 1, 1, True)

            def link(n):
                eng.wait_ge(s["gate"], n)

            eng.wait_ge(s["sumD"], 16)
            eng.reciprocal(recip[:, :], recip[:, :]).then_inc(s["recD"], 1)
            with eng.Fori(0, G) as g:
                cs = bass.ds(g * GT, GT)
                bs = bass.ds(g * GB, GB)
                for h in range(H):
                    at = (h % HH) * S
                    u = AU[0:C1, bs, h // HH, at:at + S]
                    n = H * g + h
                    eng.wait_ge(s["bcD"], n + 1)
                    if h >= 2:
                        eng.wait_ge(s["yh"], n - 1)
                    eng.tensor_tensor(un[h % 2][0:C, :].rearrange("p (b q) -> p b q", b=GB), u[0:C],
                                      ps[0:C, h % 2, 0:GT].rearrange("p (b q) -> p b q", b=GB), ALU.mult)\
                       .then_inc(s["unD"], 1)
                eng.wait_ge(s["ydD"], g + 1)
                eng.scalar_tensor_tensor(xT[:, cs], ydm, sc[:, 1:2], xT[:, cs], ALU.mult, ALU.add)\
                   .then_inc(s["xD"], 1)
                eng.wait_ge(s["xD"], g + 1)
                layer_norm(4 * G + g, xT[:, cs])

                n0 = NGATE * g
                n = [0]

                def done(ins):
                    n[0] += 1
                    ins.then_inc(s["gate"], 1)
                    eng.wait_ge(s["gate"], n0 + n[0])
                te = lambda t: t.rearrange("p (t e) -> p t e", t=NT)
                eng.wait_ge(s["ge"], g + 1)
                done(eng.tensor_scalar(gw["e1"], gw["e1"], 1.0, None, ALU.add))
                done(eng.reciprocal(gw["sc"], gw["e1"]))
                done(eng.tensor_tensor(te(gw["sfc"]), te(gw["sc"]),
                                       sc[0:MT, 7:7 + NE].unsqueeze(1).to_broadcast([MT, NT, NE]), ALU.add))

                def ranks(v, rank, k, m):
                    v = v.rearrange("p (k m) -> p k m", k=k)
                    sh = [MT, k, m, m]
                    other = v.unsqueeze(2).to_broadcast(sh)
                    own = v.unsqueeze(3).to_broadcast(sh)
                    gt = gw["gt"][:, 0:k * m * m].rearrange("p (k e j) -> p k e j", k=k, e=m)
                    eq = gw["eq"][:, 0:k * m * m].rearrange("p (k e j) -> p k e j", k=k, e=m)
                    done(eng.tensor_tensor(gt, other, own, ALU.is_gt))
                    done(eng.tensor_tensor(eq, other, own, ALU.is_equal))
                    done(eng.tensor_tensor(eq, eq, lower[:, 0:m, 0:m].unsqueeze(1).to_broadcast(sh), ALU.mult))
                    done(eng.tensor_tensor(gt, gt, eq, ALU.add))
                    done(eng.tensor_reduce(rank.rearrange("p (k m) -> p k m", k=k), gt, AX.X, ALU.add))

                ranks(gw["sfc"], gw["rank"], 16, 4)
                done(eng.scalar_tensor_tensor(gw["sel"], gw["rank"], 1.5, gw["sfc"], ALU.is_lt, ALU.mult))
                done(eng.tensor_reduce(gw["top"], gw["sel"].rearrange("p (k e) -> p k e", e=4), AX.X, ALU.add))
                ranks(gw["top"], gw["grank"], 4, 4)
                done(eng.tensor_scalar(gw["gm"], gw["grank"], 1.5, None, ALU.is_lt))
                done(eng.tensor_tensor(gw["msk"].rearrange("p (k e) -> p k e", e=4),
                                       gw["sfc"].rearrange("p (k e) -> p k e", e=4),
                                       gw["gm"].unsqueeze(2).to_broadcast([MT, 16, 4]), ALU.mult))
                ranks(gw["msk"], gw["rank"], 4, 16)
                done(eng.scalar_tensor_tensor(gw["w"], gw["rank"], 3.5, gw["msk"], ALU.is_lt, ALU.mult))
                done(eng.tensor_reduce(gw["ws"], te(gw["w"]), AX.X, ALU.add))
                done(eng.tensor_scalar(gw["ws"], gw["ws"], 1e-20, None, ALU.add))
                done(eng.reciprocal(gw["r"], gw["ws"]))
                done(eng.scalar_tensor_tensor(te(gw["comb"]), te(gw["w"]), 2.5,
                                              gw["r"].unsqueeze(2).to_broadcast([MT, NT, NE]), ALU.mult, ALU.mult))
                assert n[0] == NGATE
                eng.wait_ge(s["cT"], g + 1)
                eng.tensor_copy(combT, ps[0:NE, 6, 0:GT]).then_inc(s["cTs"], 1)

                for i, p in enumerate(ORDER):
                    m = (NP + 1) * g + i
                    bg, bu, bc = 3 * (i % 2), 3 * (i % 2) + 1, 3 * (i % 2) + 2
                    eng.wait_ge(s["th"], m + 1)
                    eng.scalar_tensor_tensor(zg[i % 2], tnh[i % 2], 1.0, ps[:, bg, 0:GT], ALU.add, ALU.mult)\
                       .then_inc(s["zg"], 1)
                    eng.wait_ge(s["zg"], m + 1)
                    if p == NP:
                        eng.scalar_tensor_tensor(inter[i % 2], ps[:, bu, 0:GT], 0.5, zg[i % 2], ALU.mult, ALU.mult)\
                           .then_inc(s["moe"], 1)
                        continue
                    eng.scalar_tensor_tensor(zu[i % 2], ps[:, bu, 0:GT], 0.5, zg[i % 2], ALU.mult, ALU.mult)\
                       .then_inc(s["zu"], 1)
                    eng.wait_ge(s["zu"], NP * g + i)
                    eng.wait_ge(s["cw"], NP * g + i)
                    if i >= 2:
                        eng.wait_ge(s["dn"], m - 1)
                    eng.tensor_tensor(inter[i % 2], zu[i % 2], ps[:, bc, 0:GT], ALU.mult).then_inc(s["moe"], 1)
                eng.wait_ge(s["dn"], (NP + 1) * g + NP + 1)
                eng.scalar_tensor_tensor(xn[:, :], ps[:, 7, 0:GT], sc[:, 3:4], xT[:, cs], ALU.mult, ALU.add)\
                   .then_inc(s["fin"], 1)

        @block.tensor
        def _(eng):
            eng.wait_ge(s["w_in"], NL)
            eng.wait_ge(s["const"], 23)
            n = [0]

            def give():
                n[0] += 1
                wait(eng, s["prep_ev"], n[0] - 2)
                return ps[:, n[0] % 2, :]

            for t in range(4):
                b = give()
                for i in range(4 * t, min(4 * t + 4, 14)):
                    mm = eng.transpose(b[:, 128 * (i - 4 * t):128 * (i - 4 * t) + 128], xnat[:, i, :], idf[:, :])
                mm.then_inc(s["prep_pe"], 1)
            eng.wait_ge(s["gates"], 1)
            eng.matmul(give()[:, 0:7 + NE], ones[0:1, :], rows[:, :], start=True, stop=True)\
               .then_inc(s["prep_pe"], 1)
            eng.matmul(give()[:, 0:1], wv0[:, :], cols[0:C, 3:4], start=True, stop=True)\
               .then_inc(s["prep_pe"], 1)
            eng.matmul(give()[:, 0:1], wk0[:, :], cols[0:C, 3:4], start=True, stop=True)\
               .then_inc(s["prep_pe"], 1)
            eng.wait_ge(s["prep_misc"], 2)
            eng.transpose(give()[:, 0:C], wk0[:, :], idf[0:C, 0:C]).then_inc(s["prep_pe"], 1)
            for src, rows_ in ((wq1, 128), (wk1, C), (wv1, C)):
                for t in range(HH // 4):
                    b = give()
                    for i in range(4):
                        at = (4 * t + i) * 128
                        mm = eng.transpose(b[:, 128 * i:128 * i + rows_], src[:, at:at + 128], idf[0:rows_, 0:rows_])
                    mm.then_inc(s["prep_pe"], 1)
            eng.wait_ge(s["prep_ev"], 14)
            for left, right, width, rows_ in ((wqT, wkT, C, 128), (wvT, wo1, 128, C)):
                for t in range(H // 4):
                    b = give()
                    for i in range(4):
                        h = 8 * (t % 2) + t // 2 + 2 * i
                        r = slice(DH * (h % 2), DH * (h % 2) + DH)
                        mm = eng.matmul(b[0:rows_, 128 * i:128 * i + width], left[r, h // 2, :], right[r, h // 2, :],
                                        start=True, stop=True)
                    mm.then_inc(s["prep_pe"], 1)
            eng.wait_ge(s["prep_ev"], n[0])

            def layer_norm(n, src):
                eng.matmul(ps[:, 0, 0:GT], mean_w[:, :], src, start=True, stop=True).then_inc(s["ln_mean"], 1)
                eng.wait_ge(s["ln_sq"], n + 1)
                for t in range(NT):
                    mm = eng.matmul(ps[0:MT, 1, t:t + 1], sqv[:, MT * t:MT * t + MT], mean_w[:, 0:1],
                                    start=True, stop=True)
                mm.then_inc(s["ln_var"], 1)
                eng.wait_ge(s["ln_rs"], n + 1)
                for t in range(NT):
                    mm = eng.matmul(ps[:, 0, MT * t:MT * t + MT], rstd[:, t:t + 1].to_broadcast([MT, 128]),
                                    idf[0:MT, 0:MT], start=True, stop=True)
                mm.then_inc(s["ln_bc"], 1)

            with eng.Fori(0, G) as g:
                layer_norm(2 * g, xT[:, bass.ds(g * GT, GT)])
                eng.wait_ge(s["ln_xn"], 2 * g + 1)
                layer_norm(2 * g + 1, xn[:, :])
                eng.wait_ge(s["x1"], g + 1)
                eng.matmul(ps[:, 2, 0:GT], wq0[:, :], xn[:, :], start=True, stop=True).then_inc(s["q0"], 1)
                eng.wait_ge(s["qT"], g + 1)
                eng.matmul(ps[0:C1, 3, 0:GT], wkA[:, :], qT[:, :], start=True, stop=True).then_inc(s["a0"], 1)
                eng.wait_ge(s["a0lo"], g + 1)

            def fill(dst_bank, q, k, sig):
                src, ident, dt = (nat_hi[k], idb, bf16) if q < 2 else (nat_lo[k], idh, fp16)
                dst = bank16(dst_bank, dt)
                for i in range(6):
                    mm = eng.transpose(dst[0:C1, 128 * i:128 * i + KP], src[:, 6 * (q % 2) + i, 0:C1],
                                       ident[0:KP, 0:KP])
                mm.then_inc(sig, 1)

            def scores(dst, T, j, hi, lo, sig):
                eng.matmul(dst, T_hi[T][0:C1, j, :], hi, start=True, stop=False)
                eng.matmul(dst, T_lo[T][0:C1, j, :], hi, start=False, stop=False)
                mm = eng.matmul(dst, T_hi[T][0:C1, j, :], lo, start=False, stop=True)
                if sig is not None:
                    mm.then_inc(sig, 1)

            def values(dst, k, j, slot, c0, width, sig):
                hi = P[slot].bitcast(bf16)[:, 2 * c0 + 1:2 * (c0 + width):2]
                eng.matmul(dst, nat_hi[k][:, j, 0:C1], hi, start=(j == 0), stop=False)
                eng.matmul(dst, nat_lo[k][:, j, 0:C1], hi, start=False, stop=False)
                mm = eng.matmul(dst, nat_hi[k][:, j, 0:C1], P_lo[slot][:, c0:c0 + width], start=False,
                                stop=(j == J - 1))
                if sig is not None:
                    mm.then_inc(sig, 1)

            def fills_a(b, k):
                for q in range(4):
                    if q % 2 == 0:
                        eng.wait_ge(s["natA_hi" if q == 0 else "natA_lo"], b + 1)
                    wait(eng, s["fevA"], 4 * b + q - 1)
                    fill((4, 7)[q % 2], q, k, s["fillA"])

            def maxima_a(b, k):
                eng.wait_ge(s["fevA"], 4 * b + 2)
                for c in range(3):
                    wait(eng, s["redA"], 3 * b + max(c - 1, 0))
                    eng.matmul(ps[:, 5 + c % 2, 0:KC], A0_hi[0:C1, bass.ds(b * S, 128)],
                               T_hi[k][0:C1, 4 * c:4 * c + 4, 0:KP], start=True, stop=True).then_inc(s["maxA"], 1)

            def shift_a(b):
                eng.wait_ge(s["negA"], b + 1)
                wait(eng, s["rowA"], b)
                eng.transpose(bank16(2, bf16)[0:1, 0:128], mneg0[:, :], idb[:, :]).then_inc(s["mtA"], 1)

            def body_a(b, k, more):
                eng.wait_ge(s["rowA"], b + 1)
                eng.wait_ge(s["fevA"], 4 * b + 4)
                for u in range(2):
                    wait(eng, s["expA"], 2 * b + u - 1)
                    for i in range(6):
                        cs = bass.ds(b * S, S)
                        scores(ps[:, u, S * i:S * i + S], k, 6 * u + i, A0_hi[0:C1, cs], A0_lo[0:C1, cs],
                               s["qkA"] if i == 5 else None)
                if more:
                    fills_a(b + 1, 1 - k)
                    maxima_a(b + 1, 1 - k)
                wait(eng, s["uA"], b)
                for j in range(J):
                    if j % 6 == 0:
                        eng.wait_ge(s["ploA"], 2 * b + j // 6 + 1)
                    values(ps[0:C1, 3, 0:S], k, j, 2 * k + j // 6, S * (j % 6), S, s["pvA"] if j == J - 1 else None)
                if more:
                    shift_a(b + 1)
            eng.wait_ge(s["a0lo"], G)
            fills_a(0, 0)
            maxima_a(0, 0)
            shift_a(0)
            body_a(0, 0, True)
            body_a(1, 1, True)
            with eng.Fori(1, NB // 2 - 1) as i:
                for k in range(2):
                    body_a(2 * i + k, k, True)
            body_a(NB - 2, 0, True)
            body_a(NB - 1, 1, False)

            eng.wait_ge(s["invB"], 16)
            with eng.Fori(0, G) as g:
                eng.matmul(ps[0:C, 0, 0:GT], spread[:, :], U0[:, bass.ds(g * GT, GT)], start=True, stop=True)\
                   .then_inc(s["bcB"], 1)
                eng.wait_ge(s["unB"], g + 1)
                eng.matmul(ps[:, 2, 0:GT], wvA[:, :], xc[0:C, :], start=True, stop=True).then_inc(s["oB"], 1)
                eng.wait_ge(s["oTB"], g + 1)
                eng.matmul(ps[:, 3, 0:GT], wo0[:, :], qT[:, :], start=True, stop=True).then_inc(s["yB"], 1)
                eng.wait_ge(s["xB"], 2 * g + 1)
                layer_norm(2 * G + 2 * g, xT[:, bass.ds(g * GT, GT)])
                eng.wait_ge(s["xhl"], 2 * g + 2)
                for m in range(FT):
                    w = w0[:, 128 * m:128 * m + 128]
                    eng.matmul(ps[:, m, 0:GT], w, xh[:, :], start=True, stop=False)
                    eng.matmul(ps[:, m, 0:GT], w, xl[:, :], start=False, stop=True).then_inc(s["h1"], 1)
                for m in range(FT):
                    for k in range(FT):
                        if m == 0:
                            eng.wait_ge(s["hlo"], 2 * FT * g + k + 1)
                        w = w1[:, k, 128 * m:128 * m + 128]
                        eng.matmul(ps[:, 4 + m, 0:GT], w, hf[:, k, :].bitcast(bf16)[:, 1:2 * GT:2],
                                   start=(k == 0), stop=False)
                        mm = eng.matmul(ps[:, 4 + m, 0:GT], w, hlo[:, k, :], start=False, stop=(k == FT - 1))
                    mm.then_inc(s["h2"], 1)
                for k in range(FT):
                    eng.wait_ge(s["hlo"], 2 * FT * g + FT + k + 1)
                    eng.matmul(ps[:, 0, 0:GT], w2[:, k, :], hf[:, k, :].bitcast(bf16)[:, 1:2 * GT:2],
                               start=(k == 0), stop=False)
                    mm = eng.matmul(ps[:, 0, 0:GT], w2[:, k, :], hlo[:, k, :], start=False, stop=(k == FT - 1))
                mm.then_inc(s["h3"], 1)
                eng.wait_ge(s["xB"], 2 * g + 2)
                layer_norm(2 * G + 2 * g + 1, xT[:, bass.ds(g * GT, GT)])
                eng.wait_ge(s["ln_xn"], 2 * G + 2 * g + 2)
                for h in range(H):
                    if h >= 4:
                        eng.wait_ge(s["alo"], H * g + h - 3)
                    eng.matmul(ps[0:C, h % 4, 0:GT], Mh[:, h, :], xn[:, :], start=True, stop=True)\
                       .then_inc(s["aq"], 1)
                eng.wait_ge(s["alo"], H * g + H)

            def fill_c(b, q, k):
                if q % 2 == 0:
                    eng.wait_ge(s["natC_hi" if q == 0 else "natC_lo"], b + 1)
                wait(eng, s["fevC"], 4 * b + q)
                fill(7, q, k, s["fillC"])

            def maximum(b, h, k, n):
                g = 2 * b + h
                if n == 0:
                    wait(eng, s["rowC"], g)
                    eng.wait_ge(s["fevC"], 4 * b + 2)
                wait(eng, s["redC"], J * g + n - 1)
                t, c = n // 3, n % 3
                eng.matmul(ps[0:MT, 5 + n % 2, 0:KC], AUhi[0:C, b, h, MT * t:MT * t + MT],
                           T_hi[k][0:C, 4 * c:4 * c + 4, 0:KP], start=True, stop=True).then_inc(s["maxC"], 1)

            def shift_c(g):
                eng.wait_ge(s["negC"], g + 1)
                for t in range(NT):
                    mm = eng.transpose(bank16(5, bf16)[0:1, MT * t:MT * t + MT], mneg[:, t:t + 1],
                                       idb[0:MT, 0:MT])
                mm.then_inc(s["mtC"], 1)

            def qk(b, k, u):
                h, j = u // J, u % J
                if j == 0:
                    eng.wait_ge(s["rowC"], 2 * b + h + 1)
                    eng.wait_ge(s["fevC"], 4 * b + 4)
                wait(eng, s["expC"], UN * b + u - 2)
                scores(ps[:, u % 3, 0:HQ], k, j, AUhi[0:C1, b, h, 0:HQ], AUlo[0:C1, b, h, HQ:2 * HQ], s["qkC"])

            def body_c(b, k, last):
                for u in range(UN):
                    h, j = u // J, u % J
                    if u + 2 < UN:
                        qk(b, k, u + 2)
                    elif not last:
                        qk(b + 1, 1 - k, u + 2 - UN)
                    if h == 0 or not last:
                        for n in MAXAT[j]:
                            maximum(b + h, 1 - h, (k + h) % 2, n)
                    if j == 0:
                        wait(eng, s["uC"], 2 * b + h - 1)
                    eng.wait_ge(s["ploC"], UN * b + u + 1)
                    values(ps[0:C1, 3 + h, 0:HQ], k, j, u % 4, 0, HQ, s["pvC"])
                    if 4 <= u < 8 and not last:
                        fill_c(b + 1, u - 4, 1 - k)
                    if j == 8 and (h == 0 or not last):
                        shift_c(2 * b + h + 1)
            eng.wait_ge(s["alo"], H * G)
            for q in range(4):
                fill_c(0, q, 0)
            for n in range(J):
                maximum(0, 0, 0, n)
            shift_c(0)
            qk(0, 0, 0)
            qk(0, 0, 1)
            body_c(0, 0, False)
            with eng.Fori(0, NB // 2 - 1) as i:
                body_c(2 * i + 1, 1, False)
                body_c(2 * i + 2, 0, False)
            body_c(NB - 1, 1, True)

            eng.wait_ge(s["invD"], 16)
            eng.wait_ge(s["sel"], 3)
            with eng.Fori(0, G) as g:
                def spread_row(h):
                    if h >= 2:
                        eng.wait_ge(s["unD"], H * g + h - 1)
                    at = (h % HH) * S
                    eng.matmul(ps[0:C, h % 2, 0:GT], spread[:, :],
                               AU[0:C1, bass.ds(g * GB, GB), h // HH, at:at + S], start=True, stop=True)\
                       .then_inc(s["bcD"], 1)
                spread_row(0)
                for h in range(H):
                    if h + 1 < H:
                        spread_row(h + 1)
                    eng.wait_ge(s["unD"], H * g + h + 1)
                    mm = eng.matmul(ps[:, 4, 0:GT], Nh[:, h, :], un[h % 2][0:C, :], start=(h == 0), stop=(h == H - 1))
                    mm.then_inc(s["yh"], 1)
                eng.wait_ge(s["xD"], g + 1)
                layer_norm(4 * G + g, xT[:, bass.ds(g * GT, GT)])
                eng.wait_ge(s["ln_xn"], 4 * G + g + 1)
                for t in range(NT):
                    mm = eng.matmul(ps[0:MT, 6, NE * t:NE * t + NE], xn[:, MT * t:MT * t + MT], gk[:, :],
                                    start=True, stop=True)
                mm.then_inc(s["lg"], 1)

                def gate_up(i):
                    m, p = (NP + 1) * g + i, ORDER[i]
                    if i >= 2:
                        eng.wait_ge(s["moe"], m - 1)
                    wgp = wg[:, 2 * p:2 * p + 2, :].rearrange("d e m -> d (e m)") if p < NP else sg[:, :]
                    wup = wu[:, 2 * p:2 * p + 2, :].rearrange("d e m -> d (e m)") if p < NP else su[:, :]
                    eng.matmul(ps[:, 3 * (i % 2), 0:GT], wgp, xn[:, :], start=True, stop=True)
                    eng.matmul(ps[:, 3 * (i % 2) + 1, 0:GT], wup, xn[:, :], start=True, stop=True)\
                       .then_inc(s["gu"], 1)

                def weights(i):
                    eng.wait_ge(s["cTs"], g + 1)
                    eng.matmul(ps[:, 3 * (i % 2) + 2, 0:GT], pairsel[:, ORDER[i], :], combT, start=True, stop=True)\
                       .then_inc(s["cw"], 1)
                gate_up(0)
                gate_up(1)
                eng.wait_ge(s["gate"], NGATE * (g + 1))
                for t in range(NT):
                    mm = eng.transpose(ps[0:NE, 6, MT * t:MT * t + MT], gw["comb"][:, NE * t:NE * t + NE],
                                       idf[0:MT, 0:MT])
                mm.then_inc(s["cT"], 1)
                weights(1)
                for i in range(NP + 1):
                    if i + 2 < NP + 1:
                        gate_up(i + 2)
                        weights(i + 2)
                    eng.wait_ge(s["moe"], (NP + 1) * g + i + 1)
                    p = ORDER[i]
                    eng.matmul(ps[:, 7, 0:GT], wd[:, p, :] if p < NP else sd[:, :], inter[i % 2],
                               start=(i == 0), stop=(i == NP)).then_inc(s["dn"], 1)
                eng.wait_ge(s["fin"], g + 1)
                for t in range(NT):
                    mm = eng.transpose(ps[0:MT, 7, 128 * t:128 * t + 128], xn[:, MT * t:MT * t + MT], idf[:, :])
                mm.then_inc(s["tr"], 1)
                eng.wait_ge(s["ev"], g + 1)

_INS = ['x', 'ctx_768', 'g_xattn', 'g_ffn', 'L0_xattn_ln1_g', 'L0_xattn_ln1_b', 'L0_xattn_ln2_g',
        'L0_xattn_ln2_b', 'L0_xattn_Wq', 'L0_xattn_bq', 'L0_xattn_Wk', 'L0_xattn_bk', 'L0_xattn_Wv',
        'L0_xattn_bv', 'L0_xattn_Wo', 'L0_xattn_bo', 'L0_ffn_k0', 'L0_ffn_k1', 'L0_ffn_k2', 'L0_ffn_s0',
        'L0_ffn_s1', 'L0_ffn_s2', 'L1_xattn_Wq', 'L1_xattn_Wk', 'L1_xattn_Wv', 'L1_xattn_Wo', 'L1_xattn_bo',
        'L1_ffn_gate_kernel', 'L1_ffn_gate_bias', 'L1_ffn_w_gate', 'L1_ffn_w_up', 'L1_ffn_w_down',
        'L1_ffn_sw_gate', 'L1_ffn_sw_up', 'L1_ffn_sw_down']
_SHAPE = (32, 56, 128)


def kernel(**inputs):
    import numpy as _np
    import concourse.bacc as _bacc
    from concourse import mybir as _mybir
    from concourse.bass_utils import run_bass_kernel_spmd as _run

    nc = _bacc.Bacc("TRN2", target_bir_lowering=False, num_devices=1)
    arrays, args = {}, {}
    for name in _INS:
        v = _np.ascontiguousarray(inputs[name])
        if v.ndim == 0:
            v = v.reshape(1)
        arrays[f"in_{name}_dram"] = v
        args[name] = nc.dram_tensor(f"in_{name}_dram", v.shape, _mybir.dt.from_np(v.dtype),
                                    kind="ExternalInput").ap()
    out = nc.dram_tensor("out_0_dram", _SHAPE, _mybir.dt.float32, kind="ExternalOutput").ap()
    flamingo_two_layer_kernel(nc, args, out)
    r = _run(nc, [arrays], core_ids=[0])
    return r.results[0]["out_0_dram"]
```

```python
import concourse.bass as bass
from concourse import mybir
from contextlib import ExitStack


def flamingo_two_layer_kernel(nc, a, out):
    fp32, bf16, fp16, u8 = mybir.dt.float32, mybir.dt.bfloat16, mybir.dt.float16, mybir.dt.uint8
    ALU = mybir.AluOpType
    ACT = mybir.ActivationFunctionType
    AX = mybir.AxisListType

    NB, S, D = a["x"].shape
    NK, C = a["ctx_768"].shape[1:]
    C1 = C + 1
    TOK = NB * S
    G = 4
    GT = TOK // G
    GB = NB // G
    J = 12
    KP = NK // J
    H, DH = 16, 64
    HH = H // 2
    HQ = HH * S
    E0 = a["L0_xattn_Wq"].shape[1]
    MT = 112
    NT = GT // MT
    KC = NK // 3
    FF = a["L0_ffn_k1"].shape[0]
    FT = FF // 128
    NE = a["L1_ffn_w_gate"].shape[0]
    ME = a["L1_ffn_w_gate"].shape[2]
    NP = NE // 2
    EPS = 1e-05
    NGATE = 27
    FILL_AT = (4, 5, 11, 12)
    FILL_EVAC = (7, 8, 14, 15)
    LEAD = 3
    ROW_AT = 8
    AHEAD = 7
    REDUCE_AT = AHEAD + 1
    ORDER = [NP] + list(range(NP))
    UN = 2 * J
    NATW = C1 + 1

    ctx = ExitStack()
    with ctx:
        def sb(name, shape, dt=fp32):
            return ctx.enter_context(nc.sbuf_tensor(name, shape, dt))

        def sem(name):
            return ctx.enter_context(nc.semaphore(name))

        def wait(eng, s, value):
            if not isinstance(value, int) or value > 0:
                eng.wait_ge(s, value)

        ps = ctx.enter_context(nc.psum_tensor("ps", [128, 8, 512], fp32))

        def bank16(n, dt):
            return ps[:, n, :].bitcast(dt)

        AU = sb("AU", [128, NB, 2, HQ])
        AUhi = AU[:, :, :, :].bitcast(bf16)
        AUlo = AU[:, :, :, :].bitcast(fp16)
        AUflat = AU[:, :, :, :].rearrange("p b h q -> p (b h q)")
        xT = sb("xT", [128, TOK])
        xc = sb("xc", [128, GT])
        sqv = sb("sqv", [128, GT])
        rstd = sb("rstd", [MT, NT])
        xn = sb("xn", [128, GT])
        work = sb("work", [128, 2 * J * C + 4 * (J * NATW // 2) + 4 * (J * 128 // 2) + 4 * HQ + 4 * (HQ // 2)])

        def carver(flat, at):
            pos = [at]

            def carve(words, dt=fp32, rows=128):
                v = flat[0:rows, pos[0]:pos[0] + words]
                pos[0] += words
                return v if dt == fp32 else v.bitcast(dt)
            return carve

        carve = carver(work[:, :], 0)
        raw = [carve(J * C, rows=KP) for _ in range(2)]
        nat_hi = [carve(J * NATW // 2, bf16, KP).rearrange("p (j c) -> p j c", j=J) for _ in range(2)]
        nat_lo = [carve(J * NATW // 2, fp16, KP).rearrange("p (j c) -> p j c", j=J) for _ in range(2)]
        T_hi = [carve(J * 64, bf16).rearrange("p (j k) -> p j k", j=J) for _ in range(2)]
        T_lo = [carve(J * 64, fp16).rearrange("p (j k) -> p j k", j=J) for _ in range(2)]
        P = [carve(HQ, rows=KP) for _ in range(4)]
        P_lo = [carve(HQ // 2, fp16, KP) for _ in range(4)]
        carve = carver(work[:, :], 0)
        un = [carve(GT) for _ in range(2)]
        ydm = carve(GT)
        tnh = [carve(GT) for _ in range(2)]
        zg = tnh
        zu = [carve(GT) for _ in range(2)]
        inter = [carve(GT) for _ in range(2)]
        combT = carve(GT, rows=NE)
        pairsel = carve(NP * 128, rows=NE).rearrange("p (t m) -> p t m", t=NP)
        ost = carve(NT * 128, rows=MT).rearrange("p (t d) -> p t d", t=NT)
        gw = {n: carve(k, rows=MT) for n, k in dict(
            e1=64, sc=64, sfc=64, gt=1024, eq=1024, rank=64, sel=64, top=16, grank=16, gm=16,
            msk=64, w=64, ws=4, r=4, comb=64).items()}

        SLOT = 2 * HQ
        carve = carver(AUflat, 0)
        wq1 = carve(H * DH)
        wk1 = carve(H * DH, rows=C)
        wv1 = carve(H * DH, rows=C)
        wo1 = carve(HH * D).rearrange("p (t d) -> p t d", t=HH)
        wqT = carve(HH * 128).rearrange("p (t d) -> p t d", t=HH)
        wkT = carve(HH * C).rearrange("p (t c) -> p t c", t=HH)
        wvT = carve(HH * C).rearrange("p (t c) -> p t c", t=HH)
        xnat = carve(14 * 128).rearrange("p (t d) -> p t d", t=14)
        k0u = carve(2 * FF // 4, u8).rearrange("p (i f) -> p i f", i=2)
        k1u = carve(FT * FF // 4, u8).rearrange("p (i f) -> p i f", i=FT)
        k2u = carve(FT * 128 // 4, u8).rearrange("p (i f) -> p i f", i=FT)
        carve = carver(AUflat, 3 * GB * SLOT)
        U0 = carve(TOK, rows=C1)
        A0_hi = carve((TOK + 128) // 2, bf16)
        A0_lo = carve((TOK + 128) // 2, fp16)
        hf = AUflat[:, 3 * GB * SLOT + TOK:][:, 0:FT * GT].rearrange("p (m q) -> p m q", m=FT)
        hlo = carve(FT * GT // 2, fp16).rearrange("p (m q) -> p m q", m=FT)
        xh = carve(GT // 2, bf16)
        xl = carve(GT // 2, fp16)
        qT = carve(GT)
        yb = carve(GT)

        idf = sb("idf", [128, 128])
        idb = sb("idb", [128, 128], bf16)
        idh = sb("idh", [128, 128], fp16)
        mean_w = sb("mean_w", [128, 128])
        ones = sb("ones", [128, 128])
        spread = sb("spread", [C1, C])
        nhalf = sb("nhalf", [128, 1])
        lower = sb("lower", [MT, NE, NE])
        wq0 = sb("wq0", [128, E0])
        wk0 = sb("wk0", [C, E0])
        wkA = sb("wkA", [E0, C1])
        wv0 = sb("wv0", [C, E0])
        wvA = sb("wvA", [C, E0])
        bvA = sb("bvA", [E0, 1])
        wo0 = sb("wo0", [E0, D])
        Mh = sb("Mh", [D, H, C])
        Nh = sb("Nh", [C, H, D])
        w0 = sb("w0", [128, FF], bf16)
        w1 = sb("w1", [128, FT, FF], bf16)
        w2 = sb("w2", [128, FT, 128], bf16)
        gk = sb("gk", [D, NE])
        wg = sb("wg", [D, NE, ME])
        wu = sb("wu", [D, NE, ME])
        wd = sb("wd", [2 * ME, NP, D])
        sg = sb("sg", [D, 2 * ME])
        su = sb("su", [D, 2 * ME])
        sd = sb("sd", [2 * ME, D])
        rows = sb("rows", [1, 7 + NE])
        sc = sb("sc", [128, 7 + NE])
        sx = sb("sx", [128, 4])
        cols = sb("cols", [128, 10])
        ln1g, ln1b, ln2g, ln2b, bq0, bk0, bo0, bo1, bv0 = (cols[:, n:n + 1] for n in range(9))
        
        st = sb("st", [KP, J, 6])
        sm = sb("sm", [KP, 6, J])
        recip = sb("recip", [128, NB * 2 * HQ // 128])
        mx = sb("mx", [MT, NT, 3])
        mneg = sb("mneg", [MT, NT], bf16)
        mx0 = sb("mx0", [S, 3])
        mneg0 = sb("mneg0", [128, 1], bf16)

        names = """w_in const prep_pe prep_ev prep_misc gates
            ln_mean ln_xc ln_sq ln_var ln_ve ln_rs ln_bc ln_xn
            x1 q0 qT a0 a0hi a0lo
            stA smA rsA x2 natA_hi natA_lo fillA fevA maxA redA negA mtA rowA qkA expA ploA pvA uA
            sumB invB sumD invD recB bcB unB oB oTB yB ybB xB xhl h1 r1 hlo h2 r2 h3 aq ahi alo zrow
            natC_hi natC_lo fillC fevC maxC redC negC mtC rowC qkC expC ploC pvC uC
            sel recD bcD unD yh yD ydD xD lg ge gate cT cTs gu th zg zu cw moe dn fin tr ev out_done""".split()
        s = {n: sem("s_" + n) for n in names}
        s_rawA = [sem(f"s_rawA{n}") for n in range(2)]
        s_rawC = [sem(f"s_rawC{n}") for n in range(2)]

        ctx_v = a["ctx_768"].rearrange("b (p j) c -> b p (j c)", j=J)

        cvec = lambda n: a[n].rearrange("(p a) -> p a", a=1)
        rvec = lambda n: a[n].rearrange("(a p) -> a p", a=1)
        loads = [
            (xnat, a["x"].rearrange("b s d -> (b s) d").rearrange("(t p) d -> p t d", p=128)),
            (wq0[:, :], a["L0_xattn_Wq"]), (wk0[:, :], a["L0_xattn_Wk"]), (wv0[:, :], a["L0_xattn_Wv"]),
            (wo0[:, :], a["L0_xattn_Wo"]), (bv0, cvec("L0_xattn_bv")),
            (ln1g, cvec("L0_xattn_ln1_g")), (ln1b, cvec("L0_xattn_ln1_b")),
            (cols[0:C, 2:3], cvec("L0_xattn_ln2_g")), (cols[0:C, 3:4], cvec("L0_xattn_ln2_b")),
            (bq0, cvec("L0_xattn_bq")), (bk0, cvec("L0_xattn_bk")), (bo0, cvec("L0_xattn_bo")),
            (bo1, cvec("L1_xattn_bo")),
            (rows[:, 0:2], rvec("g_xattn")), (rows[:, 2:4], rvec("g_ffn")),
            (rows[:, 4:5], rvec("L0_ffn_s0")), (rows[:, 5:6], rvec("L0_ffn_s1")), (rows[:, 6:7], rvec("L0_ffn_s2")),
            (rows[:, 7:7 + NE], rvec("L1_ffn_gate_bias")),
        ]
        loads2 = [
            (wq1, a["L1_xattn_Wq"]), (wk1, a["L1_xattn_Wk"]), (wv1, a["L1_xattn_Wv"]),
            (wo1, a["L1_xattn_Wo"].rearrange("(t p) d -> p t d", p=128)),
            (k0u, a["L0_ffn_k0"].rearrange("(i p) f -> p i f", p=128)),
            (k1u, a["L0_ffn_k1"].rearrange("(i p) f -> p i f", p=128)),
            (k2u, a["L0_ffn_k2"].rearrange("(i p) f -> p i f", p=128)),
            (gk[:, :], a["L1_ffn_gate_kernel"]),
            (wg[:, :, :], a["L1_ffn_w_gate"].rearrange("e h m -> h e m")),
            (wu[:, :, :], a["L1_ffn_w_up"].rearrange("e h m -> h e m")),
            (wd[:, :, :], a["L1_ffn_w_down"].rearrange("(t e) m h -> (e m) t h", e=2)),
            (sg[:, :], a["L1_ffn_sw_gate"]), (su[:, :], a["L1_ffn_sw_up"]), (sd[:, :], a["L1_ffn_sw_down"]),
        ]
        NL = 16 * (len(loads) + len(loads2))

        block = ctx.enter_context(nc.Block())

        @block.sync
        def _(eng):
            for dst, src in loads:
                eng.dma_start(dst, src).then_inc(s["w_in"], 16)

            def load_a(b, k):
                wait(eng, s["natA_lo"], b - 1)
                eng.dma_start(raw[k], ctx_v[b]).then_inc(s_rawA[k], 16)
            load_a(0, 0)
            load_a(1, 1)
            with eng.Fori(1, NB // 2) as i:
                for k in range(2):
                    load_a(2 * i + k, k)

            eng.wait_ge(s["uA"], NB)
            sums = U0[C:C1, :].rearrange("a (p k) -> a p k", p=128)
            eng.dma_start(recip[:, 0:TOK // 128], sums).then_inc(s["sumB"], 16)
            eng.wait_ge(s["recB"], 1)
            eng.dma_start(sums, recip[:, 0:TOK // 128]).then_inc(s["invB"], 16)

            def load_c(b, k):
                wait(eng, s["natC_lo"], b - 1)
                eng.dma_start(raw[k], ctx_v[b]).then_inc(s_rawC[k], 16)
            eng.wait_ge(s["natA_lo"], NB)
            load_c(0, 0)
            load_c(1, 1)
            with eng.Fori(1, NB // 2) as i:
                for k in range(2):
                    load_c(2 * i + k, k)

            eng.wait_ge(s["uC"], 2 * NB)
            sums = AUflat[C:C1, :].rearrange("a (p k) -> a p k", p=128)
            eng.dma_start(recip[:, :], sums).then_inc(s["sumD"], 16)
            eng.wait_ge(s["recD"], 1)
            eng.dma_start(sums, recip[:, :]).then_inc(s["invD"], 16)

            out_v = out.rearrange("b s d -> (b s) d").rearrange("(g t p) d -> g p t d", t=NT, p=MT)
            with eng.Fori(0, G) as g:
                eng.wait_ge(s["ev"], g + 1)
                eng.dma_start(out_v[g], ost).then_inc(s["out_done"], 16)
            eng.wait_ge(s["out_done"], 16 * G)

        @block.gpsimd
        def _(eng):
            n = 0
            for t, v in ((ones, 1.0), (mean_w, 1.0 / D), (nhalf, -0.5)):
                eng.memset(t[:, :], v).then_inc(s["const"], 1)
                n += 1
            for t in (idf, idb, idh):
                eng.memset(t[:, :], 0.0).then_inc(s["const"], 1)
                n += 1
            eng.memset(lower[:, :, :], 1.0).then_inc(s["const"], 1)
            eng.memset(spread[:, :], 0.0).then_inc(s["const"], 1)
            for k in range(2):
                eng.memset(nat_hi[k][:, :, C:C1], 1.0).then_inc(s["const"], 1)
                eng.memset(nat_lo[k][:, :, C:C1], 0.0).then_inc(s["const"], 1)
                eng.memset(T_hi[k], 0.0).then_inc(s["const"], 1)
                eng.memset(T_lo[k], 0.0).then_inc(s["const"], 1)
            eng.memset(mneg0[:, :], 0.0).then_inc(s["const"], 1)
            eng.memset(A0_hi[:, TOK:TOK + 128], 0.0).then_inc(s["const"], 1)
            n += 1 + 1 + 8 + 2
            eng.wait_ge(s["const"], n)
            for t in (idf, idb, idh):
                eng.affine_select(out=t[:, :], in_=t[:, :], compare_op=ALU.not_equal, fill=1.0,
                                  base=0, pattern=[[-1, 128]], channel_multiplier=1).then_inc(s["const"], 1)
            eng.affine_select(out=spread[:, :], in_=spread[:, :], compare_op=ALU.not_equal, fill=1.0,
                              base=-C, pattern=[[0, C]], channel_multiplier=1).then_inc(s["const"], 1)
            eng.affine_select(out=lower[:, :, :], in_=lower[:, :, :], compare_op=ALU.is_ge, fill=0.0,
                              base=-1, pattern=[[1, NE], [-1, NE]], channel_multiplier=0)\
               .then_inc(s["const"], 1)
            def ln_power(n):
                eng.wait_ge(s["ln_ve"], n + 1)
                eng.tensor_tensor(rstd[:, :], rstd[:, :], nhalf[0:MT, :].to_broadcast([MT, NT]), ALU.pow)\
                   .then_inc(s["ln_rs"], 1)

            with eng.Fori(0, G) as g:
                ln_power(2 * g)
                ln_power(2 * g + 1)

            def rstd_a(b):
                eng.wait_ge(s["smA"], 7 * b + 7)
                eng.tensor_tensor(sm[:, 4, :], sm[:, 4, :], nhalf[0:KP, :].to_broadcast([KP, J]), ALU.pow).then_inc(s["rsA"], 1)

            def low_part(b, k, hi, lo):
                src = raw[k].rearrange("p (j c) -> p j c", j=J)
                eng.wait_ge(hi, b + 1)
                eng.tensor_tensor(nat_lo[k][:, :, 0:C], src, nat_hi[k][:, :, 0:C], ALU.subtract)\
                   .then_inc(lo, 1)

            def prep_a(b, k):
                rstd_a(b)
                low_part(b, k, s["natA_hi"], s["natA_lo"])
            prep_a(0, 0)
            prep_a(1, 1)
            with eng.Fori(1, NB // 2) as i:
                for k in range(2):
                    prep_a(2 * i + k, k)

            for g in range(G):
                ln_power(2 * G + 2 * g)
                eng.wait_ge(s["h3"], g + 1)
                eng.memset(AU[C:C1, g * GB:g * GB + GB, :, :].rearrange("p b h q -> p (b h q)"), 0.0)\
                   .then_inc(s["zrow"], 1)
                eng.wait_ge(s["zrow"], g + 1)
                ln_power(2 * G + 2 * g + 1)

            low_part(0, 0, s["natC_hi"], s["natC_lo"])
            low_part(1, 1, s["natC_hi"], s["natC_lo"])
            with eng.Fori(1, NB // 2) as i:
                for k in range(2):
                    low_part(2 * i + k, k, s["natC_hi"], s["natC_lo"])

            eng.wait_ge(s["pvC"], UN * NB)
            eng.memset(pairsel, 1.0).then_inc(s["sel"], 1)
            eng.wait_ge(s["sel"], 1)
            eng.affine_select(out=pairsel, in_=pairsel, compare_op=ALU.is_ge, fill=0.0,
                              base=0, pattern=[[128, NP], [1, 128]], channel_multiplier=-ME)\
               .then_inc(s["sel"], 1)
            eng.wait_ge(s["sel"], 2)
            eng.affine_select(out=pairsel, in_=pairsel, compare_op=ALU.is_ge, fill=0.0,
                              base=ME - 1, pattern=[[-128, NP], [-1, 128]], channel_multiplier=ME)\
               .then_inc(s["sel"], 1)
            eng.wait_ge(s["sel"], 3)
            with eng.Fori(0, G) as g:
                ln_power(4 * G + g)

        @block.scalar
        def _(eng):
            for dst, src in loads2:
                eng.dma_start(dst, src).then_inc(s["w_in"], 16)
            eng.wait_ge(s["w_in"], NL)
            eng.activation(rows[:, 0:4], rows[:, 0:4], ACT.Tanh).then_inc(s["gates"], 1)

            def ln_square(n):
                eng.wait_ge(s["ln_xc"], n + 1)
                eng.activation(sqv[:, :], xc[:, :], ACT.Square).then_inc(s["ln_sq"], 1)

            with eng.Fori(0, G) as g:
                ln_square(2 * g)
                ln_square(2 * g + 1)
                eng.wait_ge(s["q0"], g + 1)
                eng.activation(qT[:, :], ps[:, 2, 0:GT], ACT.Identity, bias=bq0).then_inc(s["qT"], 1)
                eng.wait_ge(s["a0"], g + 1)
                eng.activation(A0_hi[0:C1, bass.ds(g * GT, GT)], ps[0:C1, 3, 0:GT], ACT.Copy)\
                   .then_inc(s["a0hi"], 1)

            def fill_evac(src_bank, q, k, sig):
                T, dt = (T_hi, bf16) if q < 2 else (T_lo, fp16)
                src = bank16(src_bank, dt)[0:C1, 0:6 * 128].rearrange("p (j k) -> p j k", j=6)
                eng.activation(T[k][0:C1, 6 * (q % 2):6 * (q % 2) + 6, 0:KP], src[:, :, 0:KP], ACT.Copy)\
                   .then_inc(sig, 1)

            def high_part(k, sig):
                eng.activation(nat_hi[k][:, :, 0:C], raw[k].rearrange("p (j c) -> p j c", j=J), ACT.Copy)\
                   .then_inc(sig, 1)

            def fill_a(b, k, q):
                eng.wait_ge(s["fillA"], 4 * b + q + 1)
                fill_evac((4, 7)[q % 2], q, k, s["fevA"])

            def high_a(b, k):
                eng.wait_ge(s["x2"], b + 1)
                wait(eng, s["pvA"], b - 1)
                high_part(k, s["natA_hi"])

            def body_a(b, k, more1, more2):
                for u in range(2):
                    eng.wait_ge(s["qkA"], 2 * b + u + 1)
                    wait(eng, s["pvA"], b - 1)
                    slot = 2 * k + u
                    eng.activation(P[slot][:, 0:6 * S], ps[0:KP, u, 0:6 * S], ACT.Exp).then_inc(s["expA"], 1)
                if more1:
                    for q in range(4):
                        fill_a(b + 1, 1 - k, q)
                eng.wait_ge(s["pvA"], b + 1)
                eng.activation(U0[:, bass.ds(b * S, S)], ps[0:C1, 3, 0:S], ACT.Copy).then_inc(s["uA"], 1)
                if more2:
                    high_a(b + 2, k)
            high_a(0, 0)
            high_a(1, 1)
            for q in range(4):
                fill_a(0, 0, q)
            body_a(0, 0, True, True)
            body_a(1, 1, True, True)
            with eng.Fori(1, NB // 2 - 1) as i:
                for k in range(2):
                    body_a(2 * i + k, k, True, True)
            body_a(NB - 2, 0, True, False)
            body_a(NB - 1, 1, False, False)

            with eng.Fori(0, G) as g:
                eng.wait_ge(s["oB"], g + 1)
                eng.activation(qT[:, :], ps[:, 2, 0:GT], ACT.Identity, bias=bvA[:, :]).then_inc(s["oTB"], 1)
                eng.wait_ge(s["yB"], g + 1)
                eng.activation(yb[:, :], ps[:, 3, 0:GT], ACT.Identity, bias=bo0).then_inc(s["ybB"], 1)
                ln_square(2 * G + 2 * g)
                for m in range(FT):
                    eng.wait_ge(s["h1"], FT * g + m + 1)
                    eng.activation(hf[:, m, :], ps[:, m, 0:GT], ACT.Relu, scale=sx[:, 0:1]).then_inc(s["r1"], 1)
                eng.wait_ge(s["h2"], g * FT + FT)
                for m in range(FT):
                    eng.activation(hf[:, m, :], ps[:, 4 + m, 0:GT], ACT.Relu, scale=sx[:, 1:2])\
                       .then_inc(s["r2"], 1)
                ln_square(2 * G + 2 * g + 1)
                for h in range(H):
                    eng.wait_ge(s["aq"], H * g + h + 1)
                    dst = AUhi[0:C, bass.ds(g * GB, GB), h // HH, (h % HH) * S:(h % HH) * S + S]
                    eng.activation(dst, ps[0:C, h % 4, 0:GT].rearrange("p (b q) -> p b q", b=GB), ACT.Copy)\
                       .then_inc(s["ahi"], 1)

            def u_evac(b, h):
                eng.wait_ge(s["pvC"], UN * b + J * (h + 1))
                eng.activation(AU[0:C1, b, h, :], ps[0:C1, 3 + h, 0:HQ], ACT.Copy).then_inc(s["uC"], 1)

            def high_c(b, k):
                eng.wait_ge(s_rawC[k], 16 * (b // 2) + 16 if isinstance(b, int) else b * 8 + (16 - 8 * k))
                wait(eng, s["pvC"], UN * (b - 1))
                high_part(k, s["natC_hi"])

            def body_c(b, k, first, last):
                for u in range(UN):
                    slot = u % 4
                    eng.wait_ge(s["qkC"], UN * b + u + 1)
                    wait(eng, s["pvC"], UN * b + u - 3)
                    eng.activation(P[slot][:, :], ps[0:KP, u % 3, 0:HQ], ACT.Exp).then_inc(s["expC"], 1)
                    if u == LEAD and not first:
                        u_evac(b - 1, 1)
                        if not last:
                            high_c(b + 1, 1 - k)
                    if u == J + LEAD:
                        u_evac(b, 0)
                    if u in FILL_EVAC and not last:
                        q = FILL_EVAC.index(u)
                        eng.wait_ge(s["fillC"], 4 * (b + 1) + q + 1)
                        fill_evac(7, q, 1 - k, s["fevC"])
            high_c(0, 0)
            high_c(1, 1)
            for q in range(4):
                eng.wait_ge(s["fillC"], q + 1)
                fill_evac(7, q, 0, s["fevC"])
            body_c(0, 0, True, False)
            with eng.Fori(0, NB // 2 - 1) as i:
                body_c(2 * i + 1, 1, False, False)
                body_c(2 * i + 2, 0, False, False)
            body_c(NB - 1, 1, False, True)
            u_evac(NB - 1, 1)

            with eng.Fori(0, G) as g:
                eng.wait_ge(s["yh"], H * g + H)
                eng.activation(ydm, ps[:, 4, 0:GT], ACT.Identity, bias=bo1).then_inc(s["ydD"], 1)
                ln_square(4 * G + g)
                eng.wait_ge(s["lg"], g + 1)
                eng.activation(gw["e1"], ps[0:MT, 6, 0:NT * NE], ACT.Exp, scale=-1.0).then_inc(s["ge"], 1)
                for i in range(NP + 1):
                    eng.wait_ge(s["gu"], (NP + 1) * g + i + 1)
                    eng.activation(tnh[i % 2], ps[:, 3 * (i % 2), 0:GT], ACT.Tanh, scale=0.5)\
                       .then_inc(s["th"], 1)
                eng.wait_ge(s["tr"], g + 1)
                eng.activation(ost, ps[0:MT, 7, :].rearrange("p (t d) -> p t d", t=NT), ACT.Copy)\
                   .then_inc(s["ev"], 1)
                eng.wait_ge(s["out_done"], 16 * g + 16)

        @block.vector
        def _(eng):
            eng.wait_ge(s["w_in"], NL)
            ev = [0]

            def take():
                eng.wait_ge(s["prep_pe"], ev[0] + 1)
                ev[0] += 1
                return ps[:, ev[0] % 2, :]

            for t in range(4):
                n = min(4, 14 - 4 * t)
                eng.tensor_copy(xT[:, 512 * t:512 * t + 128 * n], take()[:, 0:128 * n]).then_inc(s["prep_ev"], 1)
            eng.tensor_copy(sc[:, :], take()[:, 0:7 + NE]).then_inc(s["prep_ev"], 1)
            eng.tensor_tensor(bvA[:, :], take()[:, 0:1], bv0, ALU.add).then_inc(s["prep_ev"], 1)
            eng.tensor_scalar(wvA[:, :], wv0[:, :], cols[0:C, 2:3], None, ALU.mult).then_inc(s["prep_misc"], 1)
            b = take()
            eng.tensor_scalar(wkA[:, C:C1], b[:, 0:1], bk0, float(E0) ** -0.5, ALU.add, ALU.mult)\
               .then_inc(s["prep_ev"], 1)
            eng.tensor_scalar(wk0[:, :], wk0[:, :], cols[0:C, 2:3], None, ALU.mult).then_inc(s["prep_misc"], 1)
            eng.tensor_scalar(wkA[:, 0:C], take()[:, 0:C], float(E0) ** -0.5, None, ALU.mult)\
               .then_inc(s["prep_ev"], 1)
            for dst, width in ((wqT, 128), (wkT, C), (wvT, C)):
                for t in range(HH // 4):
                    v = take()[:, 0:512].rearrange("p (t c) -> p t c", t=4)
                    eng.tensor_copy(dst[:, 4 * t:4 * t + 4, :], v[:, :, 0:width]).then_inc(s["prep_ev"], 1)
            for t in range(H // 4):
                v = take()[:, :].rearrange("p (t c) -> p t c", t=4)
                h0 = 8 * (t % 2) + t // 2
                eng.tensor_scalar(Mh[:, h0:h0 + 7:2, :], v[:, :, 0:C], float(DH) ** -0.5, None, ALU.mult)\
                   .then_inc(s["prep_ev"], 1)
            for t in range(H // 4):
                v = take()[0:C, :].rearrange("p (t c) -> p t c", t=4)
                h0 = 8 * (t % 2) + t // 2
                eng.tensor_copy(Nh[:, h0:h0 + 7:2, :], v).then_inc(s["prep_ev"], 1)
            eng.tensor_tensor(w0[:, :], k0u[:, 0, :], k0u[:, 1, :], ALU.subtract).then_inc(s["prep_misc"], 1)
            eng.tensor_scalar(w1[:, :, :], k1u, 2.0, -1.0, ALU.mult, ALU.add).then_inc(s["prep_misc"], 1)
            eng.tensor_scalar(w2[:, :, :], k2u, 2.0, -1.0, ALU.mult, ALU.add).then_inc(s["prep_misc"], 1)
            eng.wait_ge(s["prep_ev"], 5)
            eng.tensor_scalar(sx[:, 0:1], sc[:, 4:5], 4.0, None, ALU.mult).then_inc(s["prep_misc"], 1)
            eng.tensor_scalar(sx[:, 1:2], sc[:, 5:6], 2.0, None, ALU.mult).then_inc(s["prep_misc"], 1)
            eng.tensor_tensor(sx[:, 2:3], sc[:, 2:3], sc[:, 6:7], ALU.mult).then_inc(s["prep_misc"], 1)
            eng.wait_ge(s["prep_ev"], ev[0])
            eng.wait_ge(s["prep_misc"], 8)

            def layer_norm(n, src):
                eng.wait_ge(s["ln_mean"], n + 1)
                eng.tensor_tensor(xc[:, :], src, ps[:, 0, 0:GT], ALU.subtract).then_inc(s["ln_xc"], 1)
                eng.wait_ge(s["ln_var"], n + 1)
                eng.tensor_scalar(rstd[:, :], ps[0:MT, 1, 0:NT], EPS, None, ALU.add).then_inc(s["ln_ve"], 1)
                eng.wait_ge(s["ln_bc"], n + 1)
                eng.tensor_tensor(xn[:, :], xc[:, :], ps[:, 0, 0:GT], ALU.mult).then_inc(s["ln_xn"], 1)
                eng.wait_ge(s["ln_xn"], n + 1)

            with eng.Fori(0, G) as g:
                cs = bass.ds(g * GT, GT)
                layer_norm(2 * g, xT[:, cs])
                layer_norm(2 * g + 1, xn[:, :])
                eng.tensor_scalar(xn[:, :], xn[:, :], ln1g, ln1b, ALU.mult, ALU.add).then_inc(s["x1"], 1)
                eng.wait_ge(s["a0hi"], g + 1)
                eng.tensor_tensor(A0_lo[0:C1, cs], ps[0:C1, 3, 0:GT], A0_hi[0:C1, cs], ALU.subtract)\
                   .then_inc(s["a0lo"], 1)
                eng.wait_ge(s["a0lo"], g + 1)

            def stats(b, k):
                eng.wait_ge(s_rawA[k], 16 * (b // 2) + 16 if isinstance(b, int) else b * 8 + (16 - 8 * k))
                src = raw[k].rearrange("p (j c) -> p j c", j=J)
                for j in range(J):
                    eng.bn_stats(st[:, j, :], src[:, j, :]).then_inc(s["stA"], 1)
                eng.wait_ge(s["stA"], J * b + J)
                eng.tensor_tensor(sm[:, 0, :], st[:, :, 1], st[:, :, 4], ALU.add).then_inc(s["smA"], 1)
                eng.tensor_tensor(sm[:, 1, :], st[:, :, 1], st[:, :, 4], ALU.subtract).then_inc(s["smA"], 1)
                eng.tensor_tensor(sm[:, 2, :], st[:, :, 2], st[:, :, 5], ALU.add).then_inc(s["smA"], 1)
                eng.wait_ge(s["smA"], 7 * b + 3)
                eng.scalar_tensor_tensor(sm[:, 3, :], sm[:, 1, :], 0.25, sm[:, 1, :], ALU.mult, ALU.mult)\
                   .then_inc(s["smA"], 1)
                eng.tensor_scalar(sm[:, 4, :], sm[:, 2, :], 1.0 / C, EPS, ALU.mult, ALU.add)\
                   .then_inc(s["smA"], 1)
                eng.tensor_scalar(sm[:, 0, :], sm[:, 0, :], 0.5, None, ALU.mult).then_inc(s["smA"], 1)
                eng.wait_ge(s["smA"], 7 * b + 6)
                eng.tensor_tensor(sm[:, 4, :], sm[:, 4, :], sm[:, 3, :], ALU.add).then_inc(s["smA"], 1)

            def normalise(b, k, chunks):
                src = raw[k].rearrange("p (j c) -> p j c", j=J)
                if chunks[0] == 0:
                    eng.wait_ge(s["rsA"], b + 1)
                for j in chunks:
                    ins = eng.tensor_scalar(src[:, j, :], src[:, j, :], sm[:, 0, j:j + 1], sm[:, 4, j:j + 1],
                                            ALU.subtract, ALU.mult)
                if chunks[-1] == J - 1:
                    ins.then_inc(s["x2"], 1)

            def maxima_a(b):
                for c in range(3):
                    eng.wait_ge(s["maxA"], 3 * b + c + 1)
                    eng.tensor_reduce(mx0[:, c:c + 1], ps[0:S, 5 + c % 2, 0:KC], AX.X, ALU.max)\
                       .then_inc(s["redA"], 1)
                eng.wait_ge(s["redA"], 3 * b + 3)
                wait(eng, s["mtA"], b)
                eng.tensor_reduce(mneg0[0:S, :], mx0[:, :], AX.X, ALU.max, negate=True).then_inc(s["negA"], 1)

            def row_a(b):
                eng.wait_ge(s["mtA"], b + 1)
                row = A0_hi[C:C1, bass.ds(b * S, S)]
                eng.tensor_tensor(row, bank16(2, bf16)[0:1, 0:S], row, ALU.add).then_inc(s["rowA"], 1)

            def body_a(b, k, more1, more2):
                if more2:
                    stats(b + 2, k)
                for u in range(2):
                    slot = 2 * k + u
                    eng.wait_ge(s["expA"], 2 * b + u + 1)
                    eng.tensor_tensor(P_lo[slot][:, 0:6 * S], P[slot][:, 0:6 * S],
                                      P[slot].bitcast(bf16)[:, 1:12 * S:2], ALU.subtract).then_inc(s["ploA"], 1)
                if more1:
                    maxima_a(b + 1)
                if more2:
                    normalise(b + 2, k, range(0, J // 2))
                if more1:
                    row_a(b + 1)
                if more2:
                    normalise(b + 2, k, range(J // 2, J))
            stats(0, 0)
            normalise(0, 0, range(J))
            stats(1, 1)
            normalise(1, 1, range(J))
            maxima_a(0)
            row_a(0)
            body_a(0, 0, True, True)
            body_a(1, 1, True, True)
            with eng.Fori(1, NB // 2 - 1) as i:
                for k in range(2):
                    body_a(2 * i + k, k, True, True)
            body_a(NB - 2, 0, True, False)
            body_a(NB - 1, 1, False, False)

            eng.wait_ge(s["sumB"], 16)
            eng.reciprocal(recip[:, 0:TOK // 128], recip[:, 0:TOK // 128]).then_inc(s["recB"], 1)
            with eng.Fori(0, G) as g:
                cs = bass.ds(g * GT, GT)
                eng.wait_ge(s["bcB"], g + 1)
                eng.tensor_tensor(xc[0:C, :], U0[0:C, cs], ps[0:C, 0, 0:GT], ALU.mult).then_inc(s["unB"], 1)
                eng.wait_ge(s["ybB"], g + 1)
                eng.scalar_tensor_tensor(xT[:, cs], yb[:, :], sc[:, 0:1], xT[:, cs], ALU.mult, ALU.add)\
                   .then_inc(s["xB"], 1)
                eng.wait_ge(s["xB"], 2 * g + 1)
                layer_norm(2 * G + 2 * g, xT[:, cs])
                eng.tensor_copy(xh[:, :], xn[:, :]).then_inc(s["xhl"], 1)
                eng.wait_ge(s["xhl"], 2 * g + 1)
                eng.tensor_tensor(xl[:, :], xn[:, :], xh[:, :], ALU.subtract).then_inc(s["xhl"], 1)
                for layer, r in (("h1", s["r1"]), ("h2", s["r2"])):
                    for m in range(FT):
                        eng.wait_ge(r, FT * g + m + 1)
                        eng.tensor_tensor(hlo[:, m, :], hf[:, m, :], hf[:, m, :].bitcast(bf16)[:, 1:2 * GT:2],
                                          ALU.subtract).then_inc(s["hlo"], 1)
                    if layer == "h1":
                        eng.wait_ge(s["h2"], FT * g + FT)
                eng.wait_ge(s["h3"], g + 1)
                eng.scalar_tensor_tensor(xT[:, cs], ps[:, 0, 0:GT], sx[:, 2:3], xT[:, cs], ALU.mult, ALU.add)\
                   .then_inc(s["xB"], 1)
                eng.wait_ge(s["xB"], 2 * g + 2)
                layer_norm(2 * G + 2 * g + 1, xT[:, cs])
                for h in range(H):
                    eng.wait_ge(s["ahi"], H * g + h + 1)
                    at = (h % HH) * S
                    bs = bass.ds(g * GB, GB)
                    eng.tensor_tensor(AUlo[0:C, bs, h // HH, HQ + at:HQ + at + S],
                                      ps[0:C, h % 4, 0:GT].rearrange("p (b q) -> p b q", b=GB),
                                      AUhi[0:C, bs, h // HH, at:at + S], ALU.subtract).then_inc(s["alo"], 1)

            def maximum(b, n):
                t, c = n // 3 % NT, n % 3
                if n % J == 0:
                    wait(eng, s["negC"], 2 * b + n // J)
                eng.wait_ge(s["maxC"], UN * b + n + 1)
                eng.tensor_reduce(mx[:, t, c:c + 1], ps[0:MT, 5 + n % 2, 0:KC], AX.X, ALU.max)\
                   .then_inc(s["redC"], 1)
                if n % J == J - 1:
                    g = 2 * b + n // J
                    eng.wait_ge(s["redC"], UN * b + n + 1)
                    wait(eng, s["mtC"], g)
                    eng.tensor_reduce(mneg[:, :], mx[:, :, :], AX.X, ALU.max, negate=True).then_inc(s["negC"], 1)

            def row_c(b, h):
                eng.wait_ge(s["mtC"], 2 * b + h + 1)
                eng.tensor_copy(AUhi[C:C1, b, h, 0:HQ], bank16(7, bf16)[0:1, 0:HQ]).then_inc(s["rowC"], 1)

            def body_c(b, k, last):
                for u in range(UN):
                    slot = u % 4
                    eng.wait_ge(s["expC"], UN * b + u + 1)
                    eng.tensor_tensor(P_lo[slot][:, :], P[slot][:, :], P[slot].bitcast(bf16)[:, 1:2 * HQ:2],
                                      ALU.subtract).then_inc(s["ploC"], 1)
                    if u == ROW_AT:
                        row_c(b, 1)
                    if u == ROW_AT + J and not last:
                        row_c(b + 1, 0)
                    if u < REDUCE_AT:
                        maximum(b, UN - REDUCE_AT + u)
                    elif not last:
                        maximum(b + 1, u - REDUCE_AT)
            eng.wait_ge(s["zrow"], G)
            for n in range(UN - REDUCE_AT):
                maximum(0, n)
                if n == J - 1:
                    row_c(0, 0)
            body_c(0, 0, False)
            with eng.Fori(0, NB // 2 - 1) as i:
                body_c(2 * i + 1, 1, False)
                body_c(2 * i + 2, 0, False)
            body_c(NB - 1, 1, True)

            def link(n):
                eng.wait_ge(s["gate"], n)

            eng.wait_ge(s["sumD"], 16)
            eng.reciprocal(recip[:, :], recip[:, :]).then_inc(s["recD"], 1)
            with eng.Fori(0, G) as g:
                cs = bass.ds(g * GT, GT)
                bs = bass.ds(g * GB, GB)
                for h in range(H):
                    at = (h % HH) * S
                    u = AU[0:C1, bs, h // HH, at:at + S]
                    n = H * g + h
                    eng.wait_ge(s["bcD"], n + 1)
                    if h >= 2:
                        eng.wait_ge(s["yh"], n - 1)
                    eng.tensor_tensor(un[h % 2][0:C, :].rearrange("p (b q) -> p b q", b=GB), u[0:C],
                                      ps[0:C, h % 2, 0:GT].rearrange("p (b q) -> p b q", b=GB), ALU.mult)\
                       .then_inc(s["unD"], 1)
                eng.wait_ge(s["ydD"], g + 1)
                eng.scalar_tensor_tensor(xT[:, cs], ydm, sc[:, 1:2], xT[:, cs], ALU.mult, ALU.add)\
                   .then_inc(s["xD"], 1)
                eng.wait_ge(s["xD"], g + 1)
                layer_norm(4 * G + g, xT[:, cs])

                n0 = NGATE * g
                n = [0]

                def done(ins):
                    n[0] += 1
                    ins.then_inc(s["gate"], 1)
                    eng.wait_ge(s["gate"], n0 + n[0])
                te = lambda t: t.rearrange("p (t e) -> p t e", t=NT)
                eng.wait_ge(s["ge"], g + 1)
                done(eng.tensor_scalar(gw["e1"], gw["e1"], 1.0, None, ALU.add))
                done(eng.reciprocal(gw["sc"], gw["e1"]))
                done(eng.tensor_tensor(te(gw["sfc"]), te(gw["sc"]),
                                       sc[0:MT, 7:7 + NE].unsqueeze(1).to_broadcast([MT, NT, NE]), ALU.add))

                def ranks(v, rank, k, m):
                    v = v.rearrange("p (k m) -> p k m", k=k)
                    sh = [MT, k, m, m]
                    other = v.unsqueeze(2).to_broadcast(sh)
                    own = v.unsqueeze(3).to_broadcast(sh)
                    gt = gw["gt"][:, 0:k * m * m].rearrange("p (k e j) -> p k e j", k=k, e=m)
                    eq = gw["eq"][:, 0:k * m * m].rearrange("p (k e j) -> p k e j", k=k, e=m)
                    done(eng.tensor_tensor(gt, other, own, ALU.is_gt))
                    done(eng.tensor_tensor(eq, other, own, ALU.is_equal))
                    done(eng.tensor_tensor(eq, eq, lower[:, 0:m, 0:m].unsqueeze(1).to_broadcast(sh), ALU.mult))
                    done(eng.tensor_tensor(gt, gt, eq, ALU.add))
                    done(eng.tensor_reduce(rank.rearrange("p (k m) -> p k m", k=k), gt, AX.X, ALU.add))

                ranks(gw["sfc"], gw["rank"], 16, 4)
                done(eng.scalar_tensor_tensor(gw["sel"], gw["rank"], 1.5, gw["sfc"], ALU.is_lt, ALU.mult))
                done(eng.tensor_reduce(gw["top"], gw["sel"].rearrange("p (k e) -> p k e", e=4), AX.X, ALU.add))
                ranks(gw["top"], gw["grank"], 4, 4)
                done(eng.tensor_scalar(gw["gm"], gw["grank"], 1.5, None, ALU.is_lt))
                done(eng.tensor_tensor(gw["msk"].rearrange("p (k e) -> p k e", e=4),
                                       gw["sfc"].rearrange("p (k e) -> p k e", e=4),
                                       gw["gm"].unsqueeze(2).to_broadcast([MT, 16, 4]), ALU.mult))
                ranks(gw["msk"], gw["rank"], 4, 16)
                done(eng.scalar_tensor_tensor(gw["w"], gw["rank"], 3.5, gw["msk"], ALU.is_lt, ALU.mult))
                done(eng.tensor_reduce(gw["ws"], te(gw["w"]), AX.X, ALU.add))
                done(eng.tensor_scalar(gw["ws"], gw["ws"], 1e-20, None, ALU.add))
                done(eng.reciprocal(gw["r"], gw["ws"]))
                done(eng.scalar_tensor_tensor(te(gw["comb"]), te(gw["w"]), 2.5,
                                              gw["r"].unsqueeze(2).to_broadcast([MT, NT, NE]), ALU.mult, ALU.mult))
                assert n[0] == NGATE
                eng.wait_ge(s["cT"], g + 1)
                eng.tensor_copy(combT, ps[0:NE, 6, 0:GT]).then_inc(s["cTs"], 1)

                for i, p in enumerate(ORDER):
                    m = (NP + 1) * g + i
                    bg, bu, bc = 3 * (i % 2), 3 * (i % 2) + 1, 3 * (i % 2) + 2
                    eng.wait_ge(s["th"], m + 1)
                    eng.scalar_tensor_tensor(zg[i % 2], tnh[i % 2], 1.0, ps[:, bg, 0:GT], ALU.add, ALU.mult)\
                       .then_inc(s["zg"], 1)
                    eng.wait_ge(s["zg"], m + 1)
                    if p == NP:
                        eng.scalar_tensor_tensor(inter[i % 2], ps[:, bu, 0:GT], 0.5, zg[i % 2], ALU.mult, ALU.mult)\
                           .then_inc(s["moe"], 1)
                        continue
                    eng.scalar_tensor_tensor(zu[i % 2], ps[:, bu, 0:GT], 0.5, zg[i % 2], ALU.mult, ALU.mult)\
                       .then_inc(s["zu"], 1)
                    eng.wait_ge(s["zu"], NP * g + i)
                    eng.wait_ge(s["cw"], NP * g + i)
                    if i >= 2:
                        eng.wait_ge(s["dn"], m - 1)
                    eng.tensor_tensor(inter[i % 2], zu[i % 2], ps[:, bc, 0:GT], ALU.mult).then_inc(s["moe"], 1)
                eng.wait_ge(s["dn"], (NP + 1) * g + NP + 1)
                eng.scalar_tensor_tensor(xn[:, :], ps[:, 7, 0:GT], sc[:, 3:4], xT[:, cs], ALU.mult, ALU.add)\
                   .then_inc(s["fin"], 1)

        @block.tensor
        def _(eng):
            eng.wait_ge(s["w_in"], NL)
            eng.wait_ge(s["const"], 23)
            n = [0]

            def give():
                n[0] += 1
                wait(eng, s["prep_ev"], n[0] - 2)
                return ps[:, n[0] % 2, :]

            for t in range(4):
                b = give()
                for i in range(4 * t, min(4 * t + 4, 14)):
                    mm = eng.transpose(b[:, 128 * (i - 4 * t):128 * (i - 4 * t) + 128], xnat[:, i, :], idf[:, :])
                mm.then_inc(s["prep_pe"], 1)
            eng.wait_ge(s["gates"], 1)
            eng.matmul(give()[:, 0:7 + NE], ones[0:1, :], rows[:, :], start=True, stop=True)\
               .then_inc(s["prep_pe"], 1)
            eng.matmul(give()[:, 0:1], wv0[:, :], cols[0:C, 3:4], start=True, stop=True)\
               .then_inc(s["prep_pe"], 1)
            eng.matmul(give()[:, 0:1], wk0[:, :], cols[0:C, 3:4], start=True, stop=True)\
               .then_inc(s["prep_pe"], 1)
            eng.wait_ge(s["prep_misc"], 2)
            eng.transpose(give()[:, 0:C], wk0[:, :], idf[0:C, 0:C]).then_inc(s["prep_pe"], 1)
            for src, rows_ in ((wq1, 128), (wk1, C), (wv1, C)):
                for t in range(HH // 4):
                    b = give()
                    for i in range(4):
                        at = (4 * t + i) * 128
                        mm = eng.transpose(b[:, 128 * i:128 * i + rows_], src[:, at:at + 128], idf[0:rows_, 0:rows_])
                    mm.then_inc(s["prep_pe"], 1)
            eng.wait_ge(s["prep_ev"], 14)
            for left, right, width, rows_ in ((wqT, wkT, C, 128), (wvT, wo1, 128, C)):
                for t in range(H // 4):
                    b = give()
                    for i in range(4):
                        h = 8 * (t % 2) + t // 2 + 2 * i
                        r = slice(DH * (h % 2), DH * (h % 2) + DH)
                        mm = eng.matmul(b[0:rows_, 128 * i:128 * i + width], left[r, h // 2, :], right[r, h // 2, :],
                                        start=True, stop=True)
                    mm.then_inc(s["prep_pe"], 1)
            eng.wait_ge(s["prep_ev"], n[0])

            def layer_norm(n, src):
                eng.matmul(ps[:, 0, 0:GT], mean_w[:, :], src, start=True, stop=True).then_inc(s["ln_mean"], 1)
                eng.wait_ge(s["ln_sq"], n + 1)
                for t in range(NT):
                    mm = eng.matmul(ps[0:MT, 1, t:t + 1], sqv[:, MT * t:MT * t + MT], mean_w[:, 0:1],
                                    start=True, stop=True)
                mm.then_inc(s["ln_var"], 1)
                eng.wait_ge(s["ln_rs"], n + 1)
                for t in range(NT):
                    mm = eng.matmul(ps[:, 0, MT * t:MT * t + MT], rstd[:, t:t + 1].to_broadcast([MT, 128]),
                                    idf[0:MT, 0:MT], start=True, stop=True)
                mm.then_inc(s["ln_bc"], 1)

            with eng.Fori(0, G) as g:
                layer_norm(2 * g, xT[:, bass.ds(g * GT, GT)])
                eng.wait_ge(s["ln_xn"], 2 * g + 1)
                layer_norm(2 * g + 1, xn[:, :])
                eng.wait_ge(s["x1"], g + 1)
                eng.matmul(ps[:, 2, 0:GT], wq0[:, :], xn[:, :], start=True, stop=True).then_inc(s["q0"], 1)
                eng.wait_ge(s["qT"], g + 1)
                eng.matmul(ps[0:C1, 3, 0:GT], wkA[:, :], qT[:, :], start=True, stop=True).then_inc(s["a0"], 1)
                eng.wait_ge(s["a0lo"], g + 1)

            def fill(dst_bank, q, k, sig):
                src, ident, dt = (nat_hi[k], idb, bf16) if q < 2 else (nat_lo[k], idh, fp16)
                dst = bank16(dst_bank, dt)
                for i in range(6):
                    mm = eng.transpose(dst[0:C1, 128 * i:128 * i + KP], src[:, 6 * (q % 2) + i, 0:C1],
                                       ident[0:KP, 0:KP])
                mm.then_inc(sig, 1)

            def scores(dst, T, j, hi, lo, sig):
                eng.matmul(dst, T_hi[T][0:C1, j, :], hi, start=True, stop=False)
                eng.matmul(dst, T_lo[T][0:C1, j, :], hi, start=False, stop=False)
                mm = eng.matmul(dst, T_hi[T][0:C1, j, :], lo, start=False, stop=True)
                if sig is not None:
                    mm.then_inc(sig, 1)

            def values(dst, k, j, slot, c0, width, sig):
                hi = P[slot].bitcast(bf16)[:, 2 * c0 + 1:2 * (c0 + width):2]
                eng.matmul(dst, nat_hi[k][:, j, 0:C1], hi, start=(j == 0), stop=False)
                eng.matmul(dst, nat_lo[k][:, j, 0:C1], hi, start=False, stop=False)
                mm = eng.matmul(dst, nat_hi[k][:, j, 0:C1], P_lo[slot][:, c0:c0 + width], start=False,
                                stop=(j == J - 1))
                if sig is not None:
                    mm.then_inc(sig, 1)

            def fill_a(b, k, q):
                eng.wait_ge(s["natA_hi" if q < 2 else "natA_lo"], b + 1)
                wait(eng, s["fevA"], 4 * b + q - 1)
                fill((4, 7)[q % 2], q, k, s["fillA"])

            def maximum_a(b, k, c):
                eng.wait_ge(s["fevA"], 4 * b + (1 if c == 0 else 2))
                wait(eng, s["redA"], 3 * b + max(c - 1, 0))
                eng.matmul(ps[:, 5 + c % 2, 0:KC], A0_hi[0:C1, bass.ds(b * S, 128)],
                           T_hi[k][0:C1, 4 * c:4 * c + 4, 0:KP], start=True, stop=True).then_inc(s["maxA"], 1)

            def shift_a(b):
                eng.wait_ge(s["negA"], b + 1)
                wait(eng, s["rowA"], b)
                eng.transpose(bank16(2, bf16)[0:1, 0:128], mneg0[:, :], idb[:, :]).then_inc(s["mtA"], 1)

            def scores_a(b, k, u):
                wait(eng, s["expA"], 2 * b + u - 1)
                for i in range(6):
                    cs = bass.ds(b * S, S)
                    scores(ps[:, u, S * i:S * i + S], k, 6 * u + i, A0_hi[0:C1, cs], A0_lo[0:C1, cs],
                           s["qkA"] if i == 5 else None)

            def values_a(b, k, u):
                if u == 0:
                    wait(eng, s["uA"], b)
                eng.wait_ge(s["ploA"], 2 * b + u + 1)
                for i in range(6):
                    values(ps[0:C1, 3, 0:S], k, 6 * u + i, 2 * k + u, S * i, S,
                           s["pvA"] if 6 * u + i == J - 1 else None)

            def body_a(b, k, more):
                eng.wait_ge(s["rowA"], b + 1)
                eng.wait_ge(s["fevA"], 4 * b + 4)
                scores_a(b, k, 0)
                scores_a(b, k, 1)
                if more:
                    fill_a(b + 1, 1 - k, 0)
                    fill_a(b + 1, 1 - k, 1)
                values_a(b, k, 0)
                if more:
                    maximum_a(b + 1, 1 - k, 0)
                    maximum_a(b + 1, 1 - k, 1)
                values_a(b, k, 1)
                if more:
                    maximum_a(b + 1, 1 - k, 2)
                    fill_a(b + 1, 1 - k, 2)
                    fill_a(b + 1, 1 - k, 3)
                    shift_a(b + 1)
            eng.wait_ge(s["a0lo"], G)
            for q in range(4):
                fill_a(0, 0, q)
            for c in range(3):
                maximum_a(0, 0, c)
            shift_a(0)
            body_a(0, 0, True)
            body_a(1, 1, True)
            with eng.Fori(1, NB // 2 - 1) as i:
                for k in range(2):
                    body_a(2 * i + k, k, True)
            body_a(NB - 2, 0, True)
            body_a(NB - 1, 1, False)

            eng.wait_ge(s["invB"], 16)
            with eng.Fori(0, G) as g:
                eng.matmul(ps[0:C, 0, 0:GT], spread[:, :], U0[:, bass.ds(g * GT, GT)], start=True, stop=True)\
                   .then_inc(s["bcB"], 1)
                eng.wait_ge(s["unB"], g + 1)
                eng.matmul(ps[:, 2, 0:GT], wvA[:, :], xc[0:C, :], start=True, stop=True).then_inc(s["oB"], 1)
                eng.wait_ge(s["oTB"], g + 1)
                eng.matmul(ps[:, 3, 0:GT], wo0[:, :], qT[:, :], start=True, stop=True).then_inc(s["yB"], 1)
                eng.wait_ge(s["xB"], 2 * g + 1)
                layer_norm(2 * G + 2 * g, xT[:, bass.ds(g * GT, GT)])
                eng.wait_ge(s["xhl"], 2 * g + 2)
                for m in range(FT):
                    w = w0[:, 128 * m:128 * m + 128]
                    eng.matmul(ps[:, m, 0:GT], w, xh[:, :], start=True, stop=False)
                    eng.matmul(ps[:, m, 0:GT], w, xl[:, :], start=False, stop=True).then_inc(s["h1"], 1)
                for m in range(FT):
                    for k in range(FT):
                        if m == 0:
                            eng.wait_ge(s["hlo"], 2 * FT * g + k + 1)
                        w = w1[:, k, 128 * m:128 * m + 128]
                        eng.matmul(ps[:, 4 + m, 0:GT], w, hf[:, k, :].bitcast(bf16)[:, 1:2 * GT:2],
                                   start=(k == 0), stop=False)
                        mm = eng.matmul(ps[:, 4 + m, 0:GT], w, hlo[:, k, :], start=False, stop=(k == FT - 1))
                    mm.then_inc(s["h2"], 1)
                for k in range(FT):
                    eng.wait_ge(s["hlo"], 2 * FT * g + FT + k + 1)
                    eng.matmul(ps[:, 0, 0:GT], w2[:, k, :], hf[:, k, :].bitcast(bf16)[:, 1:2 * GT:2],
                               start=(k == 0), stop=False)
                    mm = eng.matmul(ps[:, 0, 0:GT], w2[:, k, :], hlo[:, k, :], start=False, stop=(k == FT - 1))
                mm.then_inc(s["h3"], 1)
                eng.wait_ge(s["xB"], 2 * g + 2)
                layer_norm(2 * G + 2 * g + 1, xT[:, bass.ds(g * GT, GT)])
                eng.wait_ge(s["ln_xn"], 2 * G + 2 * g + 2)
                for h in range(H):
                    if h >= 4:
                        eng.wait_ge(s["alo"], H * g + h - 3)
                    eng.matmul(ps[0:C, h % 4, 0:GT], Mh[:, h, :], xn[:, :], start=True, stop=True)\
                       .then_inc(s["aq"], 1)
                eng.wait_ge(s["alo"], H * g + H)

            def fill_c(b, q, k):
                if q % 2 == 0:
                    eng.wait_ge(s["natC_hi" if q == 0 else "natC_lo"], b + 1)
                wait(eng, s["fevC"], 4 * b + q)
                fill(7, q, k, s["fillC"])

            def maximum(b, k, n):
                h, t, c = n // J, n // 3 % NT, n % 3
                if n == 0:
                    eng.wait_ge(s["fevC"], 4 * b + 2)
                wait(eng, s["redC"], UN * b + n - 1)
                eng.matmul(ps[0:MT, 5 + n % 2, 0:KC], AUhi[0:C, b, h, MT * t:MT * t + MT],
                           T_hi[k][0:C, 4 * c:4 * c + 4, 0:KP], start=True, stop=True).then_inc(s["maxC"], 1)

            def shift_c(b, h, filled):
                g = 2 * b + h
                eng.wait_ge(s["negC"], g + 1)
                eng.wait_ge(s["fevC"], filled)
                for t in range(NT):
                    mm = eng.transpose(bank16(7, bf16)[0:1, MT * t:MT * t + MT], mneg[:, t:t + 1],
                                       idb[0:MT, 0:MT])
                mm.then_inc(s["mtC"], 1)

            def qk(b, k, u):
                h, j = u // J, u % J
                if j == 0:
                    eng.wait_ge(s["rowC"], 2 * b + h + 1)
                    eng.wait_ge(s["fevC"], 4 * b + 4)
                wait(eng, s["expC"], UN * b + u - 2)
                scores(ps[:, u % 3, 0:HQ], k, j, AUhi[0:C1, b, h, 0:HQ], AUlo[0:C1, b, h, HQ:2 * HQ], s["qkC"])

            def body_c(b, k, last):
                for u in range(UN):
                    h, j = u // J, u % J
                    if u + LEAD < UN:
                        qk(b, k, u + LEAD)
                    elif not last:
                        qk(b + 1, 1 - k, u + LEAD - UN)
                    if u < AHEAD:
                        maximum(b, k, UN - AHEAD + u)
                    elif not last:
                        maximum(b + 1, 1 - k, u - AHEAD)
                    if j == 0:
                        wait(eng, s["uC"], 2 * b + h - 1)
                    eng.wait_ge(s["ploC"], UN * b + u + 1)
                    values(ps[0:C1, 3 + h, 0:HQ], k, j, u % 4, 0, HQ, s["pvC"])
                    if u in FILL_AT and not last:
                        fill_c(b + 1, FILL_AT.index(u), 1 - k)
                    if u == ROW_AT - 1:
                        shift_c(b, 1, 4 * b + (4 if last else 6))
                    if u == ROW_AT + J - 1 and not last:
                        shift_c(b + 1, 0, 4 * b + 8)
            eng.wait_ge(s["alo"], H * G)
            for q in range(4):
                fill_c(0, q, 0)
            for n in range(UN - AHEAD):
                maximum(0, 0, n)
                if n == J - 1:
                    shift_c(0, 0, 4)
            for u in range(LEAD):
                qk(0, 0, u)
            body_c(0, 0, False)
            with eng.Fori(0, NB // 2 - 1) as i:
                body_c(2 * i + 1, 1, False)
                body_c(2 * i + 2, 0, False)
            body_c(NB - 1, 1, True)

            eng.wait_ge(s["invD"], 16)
            eng.wait_ge(s["sel"], 3)
            with eng.Fori(0, G) as g:
                def spread_row(h):
                    if h >= 2:
                        eng.wait_ge(s["unD"], H * g + h - 1)
                    at = (h % HH) * S
                    eng.matmul(ps[0:C, h % 2, 0:GT], spread[:, :],
                               AU[0:C1, bass.ds(g * GB, GB), h // HH, at:at + S], start=True, stop=True)\
                       .then_inc(s["bcD"], 1)
                spread_row(0)
                for h in range(H):
                    if h + 1 < H:
                        spread_row(h + 1)
                    eng.wait_ge(s["unD"], H * g + h + 1)
                    mm = eng.matmul(ps[:, 4, 0:GT], Nh[:, h, :], un[h % 2][0:C, :], start=(h == 0), stop=(h == H - 1))
                    mm.then_inc(s["yh"], 1)
                eng.wait_ge(s["xD"], g + 1)
                layer_norm(4 * G + g, xT[:, bass.ds(g * GT, GT)])
                eng.wait_ge(s["ln_xn"], 4 * G + g + 1)
                for t in range(NT):
                    mm = eng.matmul(ps[0:MT, 6, NE * t:NE * t + NE], xn[:, MT * t:MT * t + MT], gk[:, :],
                                    start=True, stop=True)
                mm.then_inc(s["lg"], 1)

                def gate_up(i):
                    m, p = (NP + 1) * g + i, ORDER[i]
                    if i >= 2:
                        eng.wait_ge(s["moe"], m - 1)
                    wgp = wg[:, 2 * p:2 * p + 2, :].rearrange("d e m -> d (e m)") if p < NP else sg[:, :]
                    wup = wu[:, 2 * p:2 * p + 2, :].rearrange("d e m -> d (e m)") if p < NP else su[:, :]
                    eng.matmul(ps[:, 3 * (i % 2), 0:GT], wgp, xn[:, :], start=True, stop=True)
                    eng.matmul(ps[:, 3 * (i % 2) + 1, 0:GT], wup, xn[:, :], start=True, stop=True)\
                       .then_inc(s["gu"], 1)

                def weights(i):
                    eng.wait_ge(s["cTs"], g + 1)
                    eng.matmul(ps[:, 3 * (i % 2) + 2, 0:GT], pairsel[:, ORDER[i], :], combT, start=True, stop=True)\
                       .then_inc(s["cw"], 1)
                gate_up(0)
                gate_up(1)
                eng.wait_ge(s["gate"], NGATE * (g + 1))
                for t in range(NT):
                    mm = eng.transpose(ps[0:NE, 6, MT * t:MT * t + MT], gw["comb"][:, NE * t:NE * t + NE],
                                       idf[0:MT, 0:MT])
                mm.then_inc(s["cT"], 1)
                weights(1)
                for i in range(NP + 1):
                    if i + 2 < NP + 1:
                        gate_up(i + 2)
                        weights(i + 2)
                    eng.wait_ge(s["moe"], (NP + 1) * g + i + 1)
                    p = ORDER[i]
                    eng.matmul(ps[:, 7, 0:GT], wd[:, p, :] if p < NP else sd[:, :], inter[i % 2],
                               start=(i == 0), stop=(i == NP)).then_inc(s["dn"], 1)
                eng.wait_ge(s["fin"], g + 1)
                for t in range(NT):
                    mm = eng.transpose(ps[0:MT, 7, 128 * t:128 * t + 128], xn[:, MT * t:MT * t + MT], idf[:, :])
                mm.then_inc(s["tr"], 1)
                eng.wait_ge(s["ev"], g + 1)

_INS = ['x', 'ctx_768', 'g_xattn', 'g_ffn', 'L0_xattn_ln1_g', 'L0_xattn_ln1_b', 'L0_xattn_ln2_g',
        'L0_xattn_ln2_b', 'L0_xattn_Wq', 'L0_xattn_bq', 'L0_xattn_Wk', 'L0_xattn_bk', 'L0_xattn_Wv',
        'L0_xattn_bv', 'L0_xattn_Wo', 'L0_xattn_bo', 'L0_ffn_k0', 'L0_ffn_k1', 'L0_ffn_k2', 'L0_ffn_s0',
        'L0_ffn_s1', 'L0_ffn_s2', 'L1_xattn_Wq', 'L1_xattn_Wk', 'L1_xattn_Wv', 'L1_xattn_Wo', 'L1_xattn_bo',
        'L1_ffn_gate_kernel', 'L1_ffn_gate_bias', 'L1_ffn_w_gate', 'L1_ffn_w_up', 'L1_ffn_w_down',
        'L1_ffn_sw_gate', 'L1_ffn_sw_up', 'L1_ffn_sw_down']
_SHAPE = (32, 56, 128)


def kernel(**inputs):
    import numpy as _np
    import concourse.bacc as _bacc
    from concourse import mybir as _mybir
    from concourse.bass_utils import run_bass_kernel_spmd as _run

    nc = _bacc.Bacc("TRN2", target_bir_lowering=False, num_devices=1)
    arrays, args = {}, {}
    for name in _INS:
        v = _np.ascontiguousarray(inputs[name])
        if v.ndim == 0:
            v = v.reshape(1)
        arrays[f"in_{name}_dram"] = v
        args[name] = nc.dram_tensor(f"in_{name}_dram", v.shape, _mybir.dt.from_np(v.dtype),
                                    kind="ExternalInput").ap()
    out = nc.dram_tensor("out_0_dram", _SHAPE, _mybir.dt.float32, kind="ExternalOutput").ap()
    flamingo_two_layer_kernel(nc, args, out)
    r = _run(nc, [arrays], core_ids=[0])
    return r.results[0]["out_0_dram"]
```
